# Optimizing a Trainium2 kernel written in Bass

```python
import numpy as np
import jax
import jax.numpy as jnp

def _softmax(x, axis=-1):
    return jax.nn.softmax(x, axis=axis)

def _gelu(x):
    return jax.nn.gelu(x, approximate=True)

def _silu(x):
    return jax.nn.silu(x)

def _sigmoid(x):
    return jax.nn.sigmoid(x)

def _layernorm(x, axis=-1, eps=1e-05):
    m = jnp.mean(x, axis=axis, keepdims=True)
    v = jnp.var(x, axis=axis, keepdims=True)
    return (x - m) / jnp.sqrt(v + eps)

def _scatter_add(tgt, idx, src, axis=0):
    return tgt.at[idx].add(src)

def _segment_sum(src, seg, n):
    return jax.ops.segment_sum(src, seg, n)
kernel_name = 'mk_xattn_ffn_d4_seqx_r4_1bd638'

def setup_inputs(seed: int=0):
    np.random.seed(seed)
    _w = jnp.asarray

    def _rec_inputs():
        import jax
        import jax.numpy as jnp
        _rk = jax.random.key(seed)
        x = -0.0002928 + 1 * jax.random.normal(jax.random.fold_in(_rk, 1), (8, 256, 256), jnp.float32)
        _lenS = 256 - jax.random.randint(jax.random.fold_in(_rk, 7), (8,), 0, max(1, 256 // 4) + 1, jnp.int32)
        _lenS2 = 256 - jax.random.randint(jax.random.fold_in(_rk, 8), (8,), 0, max(1, 256 // 4) + 1, jnp.int32)
        _ctx_512P = jax.random.normal(jax.random.fold_in(_rk, 11), (8, 16, 128), jnp.float32)
        _ctx_512c = jax.random.dirichlet(jax.random.fold_in(_rk, 511), 0.3 * jnp.ones((16,), jnp.float32), (8, 256))
        _ctx_512t = jnp.einsum('bsk,bkd->bsd', _ctx_512c, _ctx_512P)
        _ctx_512t = _ctx_512t * jax.lax.rsqrt(jnp.mean(jnp.square(_ctx_512t)) + 1e-12) * 0.953939
        ctx_512 = 0.00222621 + 0.99962 * (_ctx_512t + 0.3 * jax.random.normal(jax.random.fold_in(_rk, 611), (8, 256, 128), jnp.float32))
        return (x, ctx_512)
    x, ctx_512 = _rec_inputs()

    def _L0_xattn_setup():
        import jax, jax.numpy as jnp
        import numpy as np
        H, D, C1, C2, S, M, B, W = (16, 32, 256, 128, 512, 128, 2, 4)

        def _ln(x, g, b):
            m = jnp.mean(x, -1, keepdims=True)
            v = jnp.var(x, -1, keepdims=True)
            return (x - m) * jax.lax.rsqrt(v + 1e-05) * g + b

        def _mha(x, y, wq, wk, wv, li1_w, li1_b, lnx_g, lnx_b, lny_g, lny_b, ln3_g, ln3_b, li2_w, li2_b, li3_w, li3_b, causal):
            xn = _ln(x, lnx_g, lnx_b)
            yn = _ln(y, lny_g, lny_b)
            q = jnp.einsum('bsc,hcd->bhsd', xn, wq)
            k = jnp.einsum('btc,hcd->bhtd', yn, wk)
            v = jnp.einsum('btc,hcd->bhtd', yn, wv)
            a = jax.nn.softmax(jnp.einsum('bhsd,bhtd->bhst', q, k) * D ** (-0.5), axis=-1)
            if causal:
                s, t = (a.shape[-2], a.shape[-1])
                mask = (jnp.arange(t)[None, :] > jnp.arange(s)[:, None]).astype(a.dtype)
                a = a * mask
            o = jnp.einsum('bhst,bhtd->bhsd', a, v)
            o = o.transpose(0, 2, 1, 3).reshape(x.shape[0], x.shape[1], H * D)
            x_out = x + o @ li1_w + li1_b
            h = jax.nn.gelu(_ln(x_out, ln3_g, ln3_b) @ li2_w + li2_b, approximate=False)
            return x_out + h @ li3_w + li3_b
        key = jax.random.key(seed)
        ks = iter(jax.random.split(key, 64))

        def w(shape, scale=0.02):
            return jax.random.normal(next(ks), shape, jnp.float32) * scale
        inp = {'xx': jax.random.normal(next(ks), (B, S, C1), jnp.float32), 'ee': jax.random.normal(next(ks), (B, M, C2), jnp.float32), 'ln1_g': jnp.ones(C1, jnp.float32), 'ln1_b': jnp.zeros(C1, jnp.float32), 'ln2_g': jnp.ones(C1, jnp.float32), 'ln2_b': jnp.zeros(C1, jnp.float32)}
        for pfx, cy in (('a1', C1), ('a2', C2)):
            inp[pfx + '_wq'] = w((H, C1, D))
            inp[pfx + '_wk'] = w((H, cy, D))
            inp[pfx + '_wv'] = w((H, cy, D))
            inp[pfx + '_li1_w'] = w((H * D, C1))
            inp[pfx + '_li1_b'] = jnp.zeros(C1, jnp.float32)
            inp[pfx + '_lnx_g'] = jnp.ones(C1, jnp.float32)
            inp[pfx + '_lnx_b'] = jnp.zeros(C1, jnp.float32)
            inp[pfx + '_lny_g'] = jnp.ones(cy, jnp.float32)
            inp[pfx + '_lny_b'] = jnp.zeros(cy, jnp.float32)
            inp[pfx + '_ln3_g'] = jnp.ones(C1, jnp.float32)
            inp[pfx + '_ln3_b'] = jnp.zeros(C1, jnp.float32)
            inp[pfx + '_li2_w'] = w((C1, C1 * W))
            inp[pfx + '_li2_b'] = jnp.zeros(C1 * W, jnp.float32)
            inp[pfx + '_li3_w'] = w((C1 * W, C1))
            inp[pfx + '_li3_b'] = jnp.zeros(C1, jnp.float32)
        inp['training'] = 0
        return inp
    _L0_xattn_all = _L0_xattn_setup()
    _L0_xattn_in = {k: v for k, v in _L0_xattn_all.items() if k in ('ln1_g', 'ln1_b', 'ln2_g', 'ln2_b', 'a1_wq', 'a1_wk', 'a1_wv', 'a1_li1_w', 'a1_li1_b', 'a1_lnx_g', 'a1_lnx_b', 'a1_lny_g', 'a1_lny_b', 'a1_ln3_g', 'a1_ln3_b', 'a1_li2_w', 'a1_li2_b', 'a1_li3_w', 'a1_li3_b', 'a2_wq', 'a2_wk', 'a2_wv', 'a2_li1_w', 'a2_li1_b', 'a2_lnx_g', 'a2_lnx_b', 'a2_lny_g', 'a2_lny_b', 'a2_ln3_g', 'a2_ln3_b', 'a2_li2_w', 'a2_li2_b', 'a2_li3_w', 'a2_li3_b')}
    del _L0_xattn_all

    def _L0_ffn_setup():
        import jax, jax.numpy as jnp
        import numpy as np
        EMBED = 256
        D_FF = 4 * EMBED
        N_EXPERTS = 8
        TOP_K = 2
        B, S = (2, 256)
        key = jax.random.key(seed)
        ks = jax.random.split(key, 10)
        sc_d = 1.0 / np.sqrt(EMBED)
        sc_h = 1.0 / np.sqrt(D_FF)
        return {'inputs': jax.random.normal(ks[0], (B, S, EMBED), jnp.float32), 'rw1': jax.random.normal(ks[1], (EMBED, D_FF), jnp.float32) * sc_d, 'rb1': jnp.zeros((D_FF,), jnp.float32), 'rw2': jax.random.normal(ks[2], (D_FF, N_EXPERTS), jnp.float32) * sc_h, 'rb2': jnp.zeros((N_EXPERTS,), jnp.float32), 'W1': jax.random.normal(ks[3], (N_EXPERTS, EMBED, D_FF), jnp.float32) * sc_d, 'b1': jnp.zeros((N_EXPERTS, D_FF), jnp.float32), 'W2': jax.random.normal(ks[4], (N_EXPERTS, D_FF, EMBED), jnp.float32) * sc_h, 'b2': jnp.zeros((N_EXPERTS, EMBED), jnp.float32)}
    _L0_ffn_all = _L0_ffn_setup()
    _L0_ffn_in = {k: v for k, v in _L0_ffn_all.items() if k in ('rw1', 'rb1', 'rw2', 'rb2', 'W1', 'b1', 'W2', 'b2')}
    del _L0_ffn_all

    def _L1_xattn_setup():
        import jax, jax.numpy as jnp
        import numpy as np
        DIM = 256
        LATENT_DIM = 128
        NUM_HEADS = 16
        HEAD_DIM = DIM // NUM_HEADS
        SCALE = HEAD_DIM ** (-0.5)
        key = jax.random.key(seed)
        k1, k2, k3, k4, k5 = jax.random.split(key, 5)
        B, xN, zN = (2, 512, 512)
        x = jax.random.normal(k1, (B, xN, DIM), dtype=jnp.float32)
        z = jax.random.normal(k2, (B, zN, LATENT_DIM), dtype=jnp.float32)
        Wq = jax.random.normal(k3, (DIM, DIM), dtype=jnp.float32) * DIM ** (-0.5)
        Wkv = jax.random.normal(k4, (2 * DIM, LATENT_DIM), dtype=jnp.float32) * LATENT_DIM ** (-0.5)
        Wo = jax.random.normal(k5, (DIM, DIM), dtype=jnp.float32) * DIM ** (-0.5)
        return {'x': x, 'z': z, 'Wq': Wq, 'Wkv': Wkv, 'Wo': Wo}
    _L1_xattn_all = _L1_xattn_setup()
    _L1_xattn_in = {k: v for k, v in _L1_xattn_all.items() if k in ('Wq', 'Wkv', 'Wo')}
    del _L1_xattn_all

    def _L1_ffn_setup():
        import jax, jax.numpy as jnp
        import numpy as np
        DIM = 256
        DEPTH = 7
        PAR = 8
        N_NODES = 2 ** (DEPTH + 1) - 1
        WIDTH = PAR * N_NODES
        key = jax.random.key(seed)
        k1, k2, k3, k4 = jax.random.split(key, 4)
        init_k = float(np.sqrt(1.0 / DIM))
        init_k2 = float(np.sqrt(1.0 / ((DEPTH + 1) * PAR)))
        oldx = jax.random.normal(k1, (4, 512, DIM), dtype=jnp.float32)
        W_in = jax.random.uniform(k2, (WIDTH, DIM), jnp.float32, -init_k, init_k)
        b_in = jax.random.uniform(k3, (WIDTH,), jnp.float32, -init_k, init_k)
        W_out = jax.random.uniform(k4, (DIM, WIDTH), jnp.float32, -init_k2, init_k2)
        return {'oldx': oldx, 'W_in': W_in, 'b_in': b_in, 'W_out': W_out}
    _L1_ffn_all = _L1_ffn_setup()
    _L1_ffn_in = {k: v for k, v in _L1_ffn_all.items() if k in ('W_in', 'b_in', 'W_out')}
    del _L1_ffn_all

    def _L2_xattn_setup():
        import jax, jax.numpy as jnp
        import numpy as np
        HEADS = 16
        D_MODEL = 256
        IMG_MODEL = 128
        D_K = D_MODEL // HEADS
        key = jax.random.key(seed)
        ks = jax.random.split(key, 12)
        B, LQ, LKV = (8, 512, 256)
        s_dm = 1.0 / np.sqrt(D_MODEL)
        s_im = 1.0 / np.sqrt(IMG_MODEL)
        return {'q': jax.random.normal(ks[0], (B, LQ, D_MODEL), jnp.float32), 'k': jax.random.normal(ks[1], (B, LKV, IMG_MODEL), jnp.float32), 'v': jax.random.normal(ks[2], (B, LKV, IMG_MODEL), jnp.float32), 'Wq': jax.random.normal(ks[3], (D_MODEL, D_MODEL), jnp.float32) * s_dm, 'bq': jnp.zeros((D_MODEL,), jnp.float32), 'Wk': jax.random.normal(ks[4], (IMG_MODEL, D_MODEL), jnp.float32) * s_im, 'bk': jnp.zeros((D_MODEL,), jnp.float32), 'Wv': jax.random.normal(ks[5], (IMG_MODEL, D_MODEL), jnp.float32) * s_im, 'bv': jnp.zeros((D_MODEL,), jnp.float32), 'Wo': jax.random.normal(ks[6], (D_MODEL, D_MODEL), jnp.float32) * s_dm, 'bo': jnp.zeros((D_MODEL,), jnp.float32)}
    _L2_xattn_all = _L2_xattn_setup()
    _L2_xattn_in = {k: v for k, v in _L2_xattn_all.items() if k in ('Wq', 'bq', 'Wk', 'bk', 'Wv', 'bv', 'Wo', 'bo')}
    del _L2_xattn_all

    def _L2_ffn_setup():
        import jax, jax.numpy as jnp
        import numpy as np
        H = 256
        I = 128
        E = 8
        TOP_K = 2
        N_SHARED = 2
        SHARED_I = I * N_SHARED
        SCALE = 2.5
        NORM_TOPK = True
        B, S = (2, 256)

        def _swiglu(x, wg, wu, wd):
            g = x @ wg.T
            u = x @ wu.T
            return jax.nn.silu(g) * u @ wd.T
        key = jax.random.key(seed)
        ks = jax.random.split(key, 8)
        std = 0.02
        return {'hidden_states': jax.random.normal(ks[0], (B, S, H), jnp.float32), 'gate_weight': jax.random.normal(ks[1], (E, H), jnp.float32) * std, 'w_gate': jax.random.normal(ks[2], (E, I, H), jnp.float32) * std, 'w_up': jax.random.normal(ks[3], (E, I, H), jnp.float32) * std, 'w_down': jax.random.normal(ks[4], (E, H, I), jnp.float32) * std, 'ws_gate': jax.random.normal(ks[5], (SHARED_I, H), jnp.float32) * std, 'ws_up': jax.random.normal(ks[6], (SHARED_I, H), jnp.float32) * std, 'ws_down': jax.random.normal(ks[7], (H, SHARED_I), jnp.float32) * std}
    _L2_ffn_all = _L2_ffn_setup()
    _L2_ffn_in = {k: v for k, v in _L2_ffn_all.items() if k in ('gate_weight', 'w_gate', 'w_up', 'w_down', 'ws_gate', 'ws_up', 'ws_down')}
    del _L2_ffn_all

    def _L3_xattn_setup():
        import jax, jax.numpy as jnp
        import numpy as np
        B, LQ, LK = (8, 512, 512)
        QD, KD, VD = (256, 128, 128)
        key = jax.random.key(seed)
        ks = jax.random.split(key, 9)
        s = 0.02
        return {'query': jax.random.normal(ks[0], (B, LQ, QD), jnp.float32), 'key': jax.random.normal(ks[1], (B, LK, KD), jnp.float32), 'value': jax.random.normal(ks[2], (B, LK, VD), jnp.float32), 'Wq': jax.random.normal(ks[3], (QD, QD), jnp.float32) * s, 'bq': jnp.zeros((QD,), jnp.float32), 'Wk': jax.random.normal(ks[4], (KD, QD), jnp.float32) * s, 'bk': jnp.zeros((QD,), jnp.float32), 'Wv': jax.random.normal(ks[5], (VD, QD), jnp.float32) * s, 'bv': jnp.zeros((QD,), jnp.float32)}
    _L3_xattn_all = _L3_xattn_setup()
    _L3_xattn_in = {k: v for k, v in _L3_xattn_all.items() if k in ('Wq', 'bq', 'Wk', 'bk', 'Wv', 'bv')}
    del _L3_xattn_all

    def _L3_ffn_setup():
        import jax, jax.numpy as jnp
        import numpy as np
        HIDDEN = 256
        INNER = 1024

        def _weight_quant(w):
            scale = 1.0 / jnp.clip(jnp.mean(jnp.abs(w)), 1e-05)
            wq = jnp.clip(jnp.round(w * scale), -1.0, 1.0) / scale
            return w + jax.lax.stop_gradient(wq - w)

        def _act_quant(x):
            scale = 127.0 / jnp.clip(jnp.max(jnp.abs(x), axis=-1, keepdims=True), 1e-05)
            xq = jnp.clip(jnp.round(x * scale), -128.0, 127.0) / scale
            return x + jax.lax.stop_gradient(xq - x)

        def _bitlinear(x, w):
            return jnp.einsum('bsi,oi->bso', _act_quant(x), _weight_quant(w))
        key = jax.random.key(seed)
        k0, k1, k2, k3 = jax.random.split(key, 4)
        x = jax.random.normal(k0, (4, 512, HIDDEN), dtype=jnp.float32)
        w_gate = jax.random.normal(k1, (INNER, HIDDEN), dtype=jnp.float32) / np.sqrt(HIDDEN)
        w_up = jax.random.normal(k2, (INNER, HIDDEN), dtype=jnp.float32) / np.sqrt(HIDDEN)
        w_down = jax.random.normal(k3, (HIDDEN, INNER), dtype=jnp.float32) / np.sqrt(INNER)
        return {'x': x, 'w_gate': w_gate, 'w_up': w_up, 'w_down': w_down}
    _L3_ffn_all = _L3_ffn_setup()
    _L3_ffn_in = {k: v for k, v in _L3_ffn_all.items() if k in ('w_gate', 'w_up', 'w_down')}
    del _L3_ffn_all
    return {'x': x, 'ctx_512': ctx_512, 'L0_xattn_ln1_g': _L0_xattn_in['ln1_g'], 'L0_xattn_ln1_b': _L0_xattn_in['ln1_b'], 'L0_xattn_ln2_g': _L0_xattn_in['ln2_g'], 'L0_xattn_ln2_b': _L0_xattn_in['ln2_b'], 'L0_xattn_a1_wq': _L0_xattn_in['a1_wq'], 'L0_xattn_a1_wk': _L0_xattn_in['a1_wk'], 'L0_xattn_a1_wv': _L0_xattn_in['a1_wv'], 'L0_xattn_a1_li1_w': _L0_xattn_in['a1_li1_w'], 'L0_xattn_a1_li1_b': _L0_xattn_in['a1_li1_b'], 'L0_xattn_a1_lnx_g': _L0_xattn_in['a1_lnx_g'], 'L0_xattn_a1_lnx_b': _L0_xattn_in['a1_lnx_b'], 'L0_xattn_a1_lny_g': _L0_xattn_in['a1_lny_g'], 'L0_xattn_a1_lny_b': _L0_xattn_in['a1_lny_b'], 'L0_xattn_a1_ln3_g': _L0_xattn_in['a1_ln3_g'], 'L0_xattn_a1_ln3_b': _L0_xattn_in['a1_ln3_b'], 'L0_xattn_a1_li2_w': _L0_xattn_in['a1_li2_w'], 'L0_xattn_a1_li2_b': _L0_xattn_in['a1_li2_b'], 'L0_xattn_a1_li3_w': _L0_xattn_in['a1_li3_w'], 'L0_xattn_a1_li3_b': _L0_xattn_in['a1_li3_b'], 'L0_xattn_a2_wq': _L0_xattn_in['a2_wq'], 'L0_xattn_a2_wk': _L0_xattn_in['a2_wk'], 'L0_xattn_a2_wv': _L0_xattn_in['a2_wv'], 'L0_xattn_a2_li1_w': _L0_xattn_in['a2_li1_w'], 'L0_xattn_a2_li1_b': _L0_xattn_in['a2_li1_b'], 'L0_xattn_a2_lnx_g': _L0_xattn_in['a2_lnx_g'], 'L0_xattn_a2_lnx_b': _L0_xattn_in['a2_lnx_b'], 'L0_xattn_a2_lny_g': _L0_xattn_in['a2_lny_g'], 'L0_xattn_a2_lny_b': _L0_xattn_in['a2_lny_b'], 'L0_xattn_a2_ln3_g': _L0_xattn_in['a2_ln3_g'], 'L0_xattn_a2_ln3_b': _L0_xattn_in['a2_ln3_b'], 'L0_xattn_a2_li2_w': _L0_xattn_in['a2_li2_w'], 'L0_xattn_a2_li2_b': _L0_xattn_in['a2_li2_b'], 'L0_xattn_a2_li3_w': _L0_xattn_in['a2_li3_w'], 'L0_xattn_a2_li3_b': _L0_xattn_in['a2_li3_b'], 'L0_ffn_rw1': _L0_ffn_in['rw1'], 'L0_ffn_rb1': _L0_ffn_in['rb1'], 'L0_ffn_rw2': _L0_ffn_in['rw2'], 'L0_ffn_rb2': _L0_ffn_in['rb2'], 'L0_ffn_W1': _L0_ffn_in['W1'], 'L0_ffn_b1': _L0_ffn_in['b1'], 'L0_ffn_W2': _L0_ffn_in['W2'], 'L0_ffn_b2': _L0_ffn_in['b2'], 'L1_xattn_Wq': _L1_xattn_in['Wq'], 'L1_xattn_Wkv': _L1_xattn_in['Wkv'], 'L1_xattn_Wo': _L1_xattn_in['Wo'], 'L1_ffn_W_in': _L1_ffn_in['W_in'], 'L1_ffn_b_in': _L1_ffn_in['b_in'], 'L1_ffn_W_out': _L1_ffn_in['W_out'], 'L2_xattn_Wq': _L2_xattn_in['Wq'], 'L2_xattn_bq': _L2_xattn_in['bq'], 'L2_xattn_Wk': _L2_xattn_in['Wk'], 'L2_xattn_bk': _L2_xattn_in['bk'], 'L2_xattn_Wv': _L2_xattn_in['Wv'], 'L2_xattn_bv': _L2_xattn_in['bv'], 'L2_xattn_Wo': _L2_xattn_in['Wo'], 'L2_xattn_bo': _L2_xattn_in['bo'], 'L2_ffn_gate_weight': _L2_ffn_in['gate_weight'], 'L2_ffn_w_gate': _L2_ffn_in['w_gate'], 'L2_ffn_w_up': _L2_ffn_in['w_up'], 'L2_ffn_w_down': _L2_ffn_in['w_down'], 'L2_ffn_ws_gate': _L2_ffn_in['ws_gate'], 'L2_ffn_ws_up': _L2_ffn_in['ws_up'], 'L2_ffn_ws_down': _L2_ffn_in['ws_down'], 'L3_xattn_Wq': _L3_xattn_in['Wq'], 'L3_xattn_bq': _L3_xattn_in['bq'], 'L3_xattn_Wk': _L3_xattn_in['Wk'], 'L3_xattn_bk': _L3_xattn_in['bk'], 'L3_xattn_Wv': _L3_xattn_in['Wv'], 'L3_xattn_bv': _L3_xattn_in['bv'], 'L3_ffn_w_gate': _L3_ffn_in['w_gate'], 'L3_ffn_w_up': _L3_ffn_in['w_up'], 'L3_ffn_w_down': _L3_ffn_in['w_down']}

def reference(x, ctx_512, L0_xattn_ln1_g, L0_xattn_ln1_b, L0_xattn_ln2_g, L0_xattn_ln2_b, L0_xattn_a1_wq, L0_xattn_a1_wk, L0_xattn_a1_wv, L0_xattn_a1_li1_w, L0_xattn_a1_li1_b, L0_xattn_a1_lnx_g, L0_xattn_a1_lnx_b, L0_xattn_a1_lny_g, L0_xattn_a1_lny_b, L0_xattn_a1_ln3_g, L0_xattn_a1_ln3_b, L0_xattn_a1_li2_w, L0_xattn_a1_li2_b, L0_xattn_a1_li3_w, L0_xattn_a1_li3_b, L0_xattn_a2_wq, L0_xattn_a2_wk, L0_xattn_a2_wv, L0_xattn_a2_li1_w, L0_xattn_a2_li1_b, L0_xattn_a2_lnx_g, L0_xattn_a2_lnx_b, L0_xattn_a2_lny_g, L0_xattn_a2_lny_b, L0_xattn_a2_ln3_g, L0_xattn_a2_ln3_b, L0_xattn_a2_li2_w, L0_xattn_a2_li2_b, L0_xattn_a2_li3_w, L0_xattn_a2_li3_b, L0_ffn_rw1, L0_ffn_rb1, L0_ffn_rw2, L0_ffn_rb2, L0_ffn_W1, L0_ffn_b1, L0_ffn_W2, L0_ffn_b2, L1_xattn_Wq, L1_xattn_Wkv, L1_xattn_Wo, L1_ffn_W_in, L1_ffn_b_in, L1_ffn_W_out, L2_xattn_Wq, L2_xattn_bq, L2_xattn_Wk, L2_xattn_bk, L2_xattn_Wv, L2_xattn_bv, L2_xattn_Wo, L2_xattn_bo, L2_ffn_gate_weight, L2_ffn_w_gate, L2_ffn_w_up, L2_ffn_w_down, L2_ffn_ws_gate, L2_ffn_ws_up, L2_ffn_ws_down, L3_xattn_Wq, L3_xattn_bq, L3_xattn_Wk, L3_xattn_bk, L3_xattn_Wv, L3_xattn_bv, L3_ffn_w_gate, L3_ffn_w_up, L3_ffn_w_down):
    import jax
    import jax.numpy as jnp

    def _L0_xattn_ref(xx, ee, ln1_g, ln1_b, ln2_g, ln2_b, a1_wq, a1_wk, a1_wv, a1_li1_w, a1_li1_b, a1_lnx_g, a1_lnx_b, a1_lny_g, a1_lny_b, a1_ln3_g, a1_ln3_b, a1_li2_w, a1_li2_b, a1_li3_w, a1_li3_b, a2_wq, a2_wk, a2_wv, a2_li1_w, a2_li1_b, a2_lnx_g, a2_lnx_b, a2_lny_g, a2_lny_b, a2_ln3_g, a2_ln3_b, a2_li2_w, a2_li2_b, a2_li3_w, a2_li3_b, training):
        import jax, jax.numpy as jnp
        import numpy as np
        H, D, C1, C2, S, M, B, W = (16, 32, 256, 128, 512, 128, 2, 4)

        def _ln(x, g, b):
            m = jnp.mean(x, -1, keepdims=True)
            v = jnp.var(x, -1, keepdims=True)
            return (x - m) * jax.lax.rsqrt(v + 1e-05) * g + b

        def _mha(x, y, wq, wk, wv, li1_w, li1_b, lnx_g, lnx_b, lny_g, lny_b, ln3_g, ln3_b, li2_w, li2_b, li3_w, li3_b, causal):
            xn = _ln(x, lnx_g, lnx_b)
            yn = _ln(y, lny_g, lny_b)
            q = jnp.einsum('bsc,hcd->bhsd', xn, wq)
            k = jnp.einsum('btc,hcd->bhtd', yn, wk)
            v = jnp.einsum('btc,hcd->bhtd', yn, wv)
            a = jax.nn.softmax(jnp.einsum('bhsd,bhtd->bhst', q, k) * D ** (-0.5), axis=-1)
            if causal:
                s, t = (a.shape[-2], a.shape[-1])
                mask = (jnp.arange(t)[None, :] > jnp.arange(s)[:, None]).astype(a.dtype)
                a = a * mask
            o = jnp.einsum('bhst,bhtd->bhsd', a, v)
            o = o.transpose(0, 2, 1, 3).reshape(x.shape[0], x.shape[1], H * D)
            x_out = x + o @ li1_w + li1_b
            h = jax.nn.gelu(_ln(x_out, ln3_g, ln3_b) @ li2_w + li2_b, approximate=False)
            return x_out + h @ li3_w + li3_b
        x = _ln(xx, ln1_g, ln1_b)
        x = x + _mha(x, x, a1_wq, a1_wk, a1_wv, a1_li1_w, a1_li1_b, a1_lnx_g, a1_lnx_b, a1_lny_g, a1_lny_b, a1_ln3_g, a1_ln3_b, a1_li2_w, a1_li2_b, a1_li3_w, a1_li3_b, causal=True)
        x = _ln(x, ln2_g, ln2_b)
        return x + _mha(x, ee, a2_wq, a2_wk, a2_wv, a2_li1_w, a2_li1_b, a2_lnx_g, a2_lnx_b, a2_lny_g, a2_lny_b, a2_ln3_g, a2_ln3_b, a2_li2_w, a2_li2_b, a2_li3_w, a2_li3_b, causal=False)

    def _L0_ffn_ref(inputs, rw1, rb1, rw2, rb2, W1, b1, W2, b2):
        import jax, jax.numpy as jnp
        import numpy as np
        EMBED = 256
        D_FF = 4 * EMBED
        N_EXPERTS = 8
        TOP_K = 2
        B, S = (2, 256)
        Bb, Ss, D = inputs.shape
        T = Bb * Ss
        xf = inputs.reshape(T, D)
        score = jax.nn.relu(xf @ rw1 + rb1) @ rw2 + rb2
        _, topi = jax.lax.top_k(score, TOP_K)
        mask = jnp.zeros(score.shape, bool).at[jnp.arange(T)[:, None], topi].set(True)
        gate = jax.nn.softmax(jnp.where(mask, score, -jnp.inf), axis=-1)
        out = jnp.zeros_like(xf)
        for e in range(N_EXPERTS):
            h = jax.nn.relu(xf @ W1[e] + b1[e])
            y = h @ W2[e] + b2[e]
            out = out + gate[:, e:e + 1] * y
        return out.reshape(Bb, Ss, D)

    def _L1_xattn_ref(x, z, Wq, Wkv, Wo):
        import jax, jax.numpy as jnp
        import numpy as np
        DIM = 256
        LATENT_DIM = 128
        NUM_HEADS = 16
        HEAD_DIM = DIM // NUM_HEADS
        SCALE = HEAD_DIM ** (-0.5)
        B, xN, _ = x.shape
        _, zN, _ = z.shape
        Q = (x @ Wq.T).reshape(B, xN, NUM_HEADS, HEAD_DIM)
        KV = (z @ Wkv.T).reshape(B, zN, 2, NUM_HEADS, HEAD_DIM)
        K = KV[:, :, 0]
        V = KV[:, :, 1]
        attn = jnp.einsum('bqhd,bkhd->bhqk', Q, K) * SCALE
        attn = jax.nn.softmax(attn, axis=-1)
        O = jnp.einsum('bhqk,bkhd->bqhd', attn, V).reshape(B, xN, DIM)
        return O @ Wo.T

    def _L1_ffn_ref(oldx, W_in, b_in, W_out):
        import jax, jax.numpy as jnp
        import numpy as np
        DIM = 256
        DEPTH = 7
        PAR = 8
        N_NODES = 2 ** (DEPTH + 1) - 1
        WIDTH = PAR * N_NODES
        x = oldx.reshape(-1, DIM)
        B = x.shape[0]
        logits = x @ W_in.T + b_in
        decisions = (logits > 0).astype(jnp.int32).reshape(B, PAR, N_NODES)
        acts = jax.nn.silu(logits).reshape(B, PAR, N_NODES)
        current = jnp.zeros((B, PAR), dtype=jnp.int32)
        dmap = jax.nn.one_hot(current, N_NODES, dtype=acts.dtype)
        for d in range(DEPTH):
            cur_platform = 2 ** d - 1
            next_platform = 2 ** (d + 1) - 1
            moves = jnp.take_along_axis(decisions, current[..., None], axis=2)[..., 0]
            current = (current - cur_platform) * 2 + moves + next_platform
            dmap = dmap + jax.nn.one_hot(current, N_NODES, dtype=acts.dtype)
        masked = acts * jax.lax.stop_gradient(dmap)
        out = masked.reshape(B, WIDTH) @ W_out.T
        return out.reshape(oldx.shape)

    def _L2_xattn_ref(q, k, v, Wq, bq, Wk, bk, Wv, bv, Wo, bo):
        import jax, jax.numpy as jnp
        import numpy as np
        HEADS = 16
        D_MODEL = 256
        IMG_MODEL = 128
        D_K = D_MODEL // HEADS
        B, LQ, _ = q.shape
        LKV = k.shape[1]
        qh = (q @ Wq + bq).reshape(B, LQ, HEADS, D_K).transpose(0, 2, 1, 3)
        kh = (k @ Wk + bk).reshape(B, LKV, HEADS, D_K).transpose(0, 2, 1, 3)
        vh = (v @ Wv + bv).reshape(B, LKV, HEADS, D_K).transpose(0, 2, 1, 3)
        scale = 1.0 / np.sqrt(D_K)
        scores = jnp.einsum('bhqd,bhkd->bhqk', qh, kh) * scale
        attn = jax.nn.softmax(scores, axis=-1)
        out = jnp.einsum('bhqk,bhkd->bhqd', attn, vh)
        concat = out.transpose(0, 2, 1, 3).reshape(B, LQ, D_MODEL)
        return concat @ Wo + bo

    def _L2_ffn_ref(hidden_states, gate_weight, w_gate, w_up, w_down, ws_gate, ws_up, ws_down):
        import jax, jax.numpy as jnp
        import numpy as np
        H = 256
        I = 128
        E = 8
        TOP_K = 2
        N_SHARED = 2
        SHARED_I = I * N_SHARED
        SCALE = 2.5
        NORM_TOPK = True
        B, S = (2, 256)

        def _swiglu(x, wg, wu, wd):
            g = x @ wg.T
            u = x @ wu.T
            return jax.nn.silu(g) * u @ wd.T
        b, s, h = hidden_states.shape
        x = hidden_states.reshape(-1, h)
        shared_out = _swiglu(x, ws_gate, ws_up, ws_down)
        logits = x.astype(jnp.float32) @ gate_weight.astype(jnp.float32).T
        scores = jax.nn.sigmoid(logits)
        topk_w, topk_idx = jax.lax.top_k(scores, TOP_K)
        if TOP_K > 1 and NORM_TOPK:
            topk_w = topk_w / (topk_w.sum(-1, keepdims=True) + 1e-20)
        topk_w = topk_w * SCALE
        onehot = jax.nn.one_hot(topk_idx, E, dtype=topk_w.dtype)
        combine = jnp.einsum('tk,tke->te', topk_w, onehot)
        g = jnp.einsum('th,eih->tei', x, w_gate)
        u = jnp.einsum('th,eih->tei', x, w_up)
        hmid = jax.nn.silu(g) * u
        y = jnp.einsum('tei,ehi->teh', hmid, w_down)
        routed_out = jnp.einsum('te,teh->th', combine, y)
        out = (routed_out + shared_out).reshape(b, s, h)
        return out

    def _L3_xattn_ref(query, key, value, Wq, bq, Wk, bk, Wv, bv):
        import jax, jax.numpy as jnp
        import numpy as np
        B, LQ, LK = (8, 512, 512)
        QD, KD, VD = (256, 128, 128)
        q = jnp.einsum('bld,de->ble', query, Wq) + bq
        k = jnp.einsum('bld,de->ble', key, Wk) + bk
        v = jnp.einsum('bld,de->ble', value, Wv) + bv
        scores = jnp.einsum('bqe,bke->bqk', q, k)
        attn = jax.nn.softmax(scores, axis=-1)
        out = jnp.einsum('bqk,bke->bqe', attn, v)
        return out

    def _L3_ffn_ref(x, w_gate, w_up, w_down):
        import jax, jax.numpy as jnp
        import numpy as np
        HIDDEN = 256
        INNER = 1024

        def _weight_quant(w):
            scale = 1.0 / jnp.clip(jnp.mean(jnp.abs(w)), 1e-05)
            wq = jnp.clip(jnp.round(w * scale), -1.0, 1.0) / scale
            return w + jax.lax.stop_gradient(wq - w)

        def _act_quant(x):
            scale = 127.0 / jnp.clip(jnp.max(jnp.abs(x), axis=-1, keepdims=True), 1e-05)
            xq = jnp.clip(jnp.round(x * scale), -128.0, 127.0) / scale
            return x + jax.lax.stop_gradient(xq - x)

        def _bitlinear(x, w):
            return jnp.einsum('bsi,oi->bso', _act_quant(x), _weight_quant(w))
        gate = jax.nn.silu(_bitlinear(x, w_gate))
        up = _bitlinear(x, w_up)
        return _bitlinear(gate * up, w_down)
    x = x + _L0_xattn_ref(_layernorm(x, axis=-1), ctx_512, L0_xattn_ln1_g, L0_xattn_ln1_b, L0_xattn_ln2_g, L0_xattn_ln2_b, L0_xattn_a1_wq, L0_xattn_a1_wk, L0_xattn_a1_wv, L0_xattn_a1_li1_w, L0_xattn_a1_li1_b, L0_xattn_a1_lnx_g, L0_xattn_a1_lnx_b, L0_xattn_a1_lny_g, L0_xattn_a1_lny_b, L0_xattn_a1_ln3_g, L0_xattn_a1_ln3_b, L0_xattn_a1_li2_w, L0_xattn_a1_li2_b, L0_xattn_a1_li3_w, L0_xattn_a1_li3_b, L0_xattn_a2_wq, L0_xattn_a2_wk, L0_xattn_a2_wv, L0_xattn_a2_li1_w, L0_xattn_a2_li1_b, L0_xattn_a2_lnx_g, L0_xattn_a2_lnx_b, L0_xattn_a2_lny_g, L0_xattn_a2_lny_b, L0_xattn_a2_ln3_g, L0_xattn_a2_ln3_b, L0_xattn_a2_li2_w, L0_xattn_a2_li2_b, L0_xattn_a2_li3_w, L0_xattn_a2_li3_b, 0)
    x = x + _L0_ffn_ref(_layernorm(x, axis=-1), L0_ffn_rw1, L0_ffn_rb1, L0_ffn_rw2, L0_ffn_rb2, L0_ffn_W1, L0_ffn_b1, L0_ffn_W2, L0_ffn_b2)
    x = x + _L1_xattn_ref(_layernorm(x, axis=-1), ctx_512, L1_xattn_Wq, L1_xattn_Wkv, L1_xattn_Wo)
    x = x + _L1_ffn_ref(_layernorm(x, axis=-1), L1_ffn_W_in, L1_ffn_b_in, L1_ffn_W_out)
    x = x + _L2_xattn_ref(_layernorm(x, axis=-1), ctx_512, ctx_512, L2_xattn_Wq, L2_xattn_bq, L2_xattn_Wk, L2_xattn_bk, L2_xattn_Wv, L2_xattn_bv, L2_xattn_Wo, L2_xattn_bo)
    x = x + _L2_ffn_ref(_layernorm(x, axis=-1), L2_ffn_gate_weight, L2_ffn_w_gate, L2_ffn_w_up, L2_ffn_w_down, L2_ffn_ws_gate, L2_ffn_ws_up, L2_ffn_ws_down)
    x = x + _L3_xattn_ref(_layernorm(x, axis=-1), ctx_512, ctx_512, L3_xattn_Wq, L3_xattn_bq, L3_xattn_Wk, L3_xattn_bk, L3_xattn_Wv, L3_xattn_bv)
    x = x + _L3_ffn_ref(_layernorm(x, axis=-1), L3_ffn_w_gate, L3_ffn_w_up, L3_ffn_w_down)
    return x

_drawn_inputs = setup_inputs


def setup_inputs(seed=0):
    import zlib

    import numpy as np

    out = dict(_drawn_inputs(seed))
    spreads = {'L0_xattn_ln1_g': (1.0, 0.2),
     'L0_xattn_ln1_b': (0.0, 0.1),
     'L0_xattn_ln2_g': (1.0, 0.2),
     'L0_xattn_ln2_b': (0.0, 0.1),
     'L0_xattn_a1_li1_b': (0.0, 0.1),
     'L0_xattn_a1_lnx_g': (1.0, 0.6),
     'L0_xattn_a1_lnx_b': (0.0, 0.8),
     'L0_xattn_a1_lny_g': (1.0, 0.6),
     'L0_xattn_a1_lny_b': (0.0, 0.65),
     'L0_xattn_a1_ln3_g': (1.0, 0.6),
     'L0_xattn_a1_ln3_b': (0.0, 0.637),
     'L0_xattn_a1_li2_b': (0.0, 0.327),
     'L0_xattn_a1_li3_b': (0.0, 0.1),
     'L0_xattn_a2_li1_b': (0.0, 0.1),
     'L0_xattn_a2_lnx_g': (1.0, 0.6),
     'L0_xattn_a2_lnx_b': (0.0, 0.8),
     'L0_xattn_a2_lny_g': (1.0, 0.6),
     'L0_xattn_a2_lny_b': (0.0, 0.8),
     'L0_xattn_a2_ln3_g': (1.0, 0.6),
     'L0_xattn_a2_ln3_b': (0.0, 0.672),
     'L0_xattn_a2_li2_b': (0.0, 0.374),
     'L0_xattn_a2_li3_b': (0.0, 0.1),
     'L0_ffn_rb1': (0.0, 0.1),
     'L0_ffn_rb2': (0.0, 0.1),
     'L0_ffn_b1': (0.0, 0.414),
     'L0_ffn_b2': (0.0, 0.302),
     'L2_xattn_bq': (0.0, 0.8),
     'L2_xattn_bk': (0.0, 2.0),
     'L2_xattn_bv': (0.0, 0.1),
     'L2_xattn_bo': (0.0, 0.1),
     'L3_xattn_bq': (0.0, 2.0),
     'L3_xattn_bk': (0.0, 2.0),
     'L3_xattn_bv': (0.0, 1.606)}
    factors = {'L0_xattn_a1_wq': 8.0,
     'L0_xattn_a1_wk': 8.0,
     'L0_xattn_a1_wv': 4.971,
     'L0_xattn_a1_li1_w': 4.5,
     'L0_xattn_a2_wq': 8.0,
     'L0_xattn_a2_wk': 8.0,
     'L1_ffn_b_in': 3.092,
     'L2_ffn_gate_weight': 8.0,
     'L2_ffn_w_gate': 8.0,
     'L2_ffn_w_up': 8.0,
     'L2_ffn_w_down': 8.0,
     'L2_ffn_ws_gate': 8.0,
     'L2_ffn_ws_up': 8.0,
     'L2_ffn_ws_down': 8.0,
     'L3_xattn_Wq': 14.843,
     'L3_xattn_Wk': 13.273,
     'L3_xattn_Wv': 4.046,
     'L3_ffn_w_gate': 6.955,
     'L3_ffn_w_up': 6.674,
     'L3_ffn_w_down': 6.692}
    for name, (base, spread) in spreads.items():
        noise = np.random.default_rng([zlib.crc32(name.encode()), seed]).standard_normal(out[name].shape)
        drawn = base * np.exp(spread * noise) if base else spread * noise
        out[name] = jnp.asarray(drawn.astype(out[name].dtype))
    for name, factor in factors.items():
        out[name] = (out[name] * factor).astype(out[name].dtype)
    return out
```

```python
from contextlib import ExitStack

import numpy as np

import concourse.bass as bass
from concourse import mybir

F32 = mybir.dt.float32
F32R = mybir.dt.float32r
BF16 = mybir.dt.bfloat16
ACT = mybir.ActivationFunctionType
ALU = mybir.AluOpType
AX = mybir.AxisListType

P = 128
C = 256
CT = C // P
B = 8
S = 256
NT = B * S // P
TB = S // P
CD = 128
HEADS = 16
HH = HEADS // 2
CHUNK = 512
CK = CHUNK // P
NCH = NT // CK
FF = 1024
FT = FF // P
SLOT = 4096
PIECE = 1024
EPS = 1e-5
E = 8
TOP = 2
TREES = 8
DEPTH = 7
TREE = 2 ** (DEPTH + 1) - 1
NODES = TREES * TREE
TREE_T = -(-NODES // P)
SWIGLU = 2 * CT * E * P + E * C + 2 * CT * C + CT * C + CT * E
GATE_SCALE = 2.5
TINY = 1e-20
LEVELS = 127.0
FLOOR = 1e-5
ROUND = 1.5 * 2.0 ** 23
KIB = 1024


class Signal:

    CREDIT = 8

    def __init__(self, sem):
        self.sem = sem
        self.base = self.CREDIT
        self.per = 0

    def begin(self, per):
        self.per = per

    def at(self, n, k):
        return n * self.per + (self.base + k)

    def end(self, passes):
        self.base += passes * self.per


class DmaSignal(Signal):

    CREDIT = 16

    def at(self, n, k):
        return n * (16 * self.per) + (self.base + 16 * k)

    def end(self, passes):
        self.base += 16 * passes * self.per


class Space:

    def __init__(self, nc, tag, ranges):
        self.nc, self.tag, self.free = nc, tag, [list(r) for r in ranges]

    def take(self, name, shape, dtype=F32):
        size = 2 if dtype == BF16 else 4
        for n in shape[1:]:
            size *= n
        size = (size + 31) // 32 * 32
        for r in self.free:
            if r[1] - r[0] >= size:
                at = r[0]
                r[0] += size
                return self.nc.alloc_sbuf_tensor_at(f"{self.tag}_{name}", shape, dtype, offset=at)
        raise ValueError(f"no room for {self.tag}_{name}: {size} of {self.free}")


def product(pe, out, left, right, start, stop):
    pe.matmul(out, left[0], right[0], start=start, stop=False)
    pe.matmul(out, left[0], right[1], start=False, stop=False)
    return pe.matmul(out, left[1], right[0], start=False, stop=stop)


class Prefetch:

    def __init__(self, kit, src, to, n, passes):
        self.kit, self.src, self.to = kit, src, to
        self.w = n // passes // 2
        self.passes = passes
        assert self.w * 2 * passes == n and self.w <= PIECE
        kit.w_split.begin(4)
        for landed in kit.w_landed:
            landed.begin(1)

    def load(self, sp, n):
        sp.wait_ge(self.kit.w_split.sem, self.kit.w_split.at(n, 0))
        for r in range(2):
            sp.dma_start(self.kit.raw[r][:, 0:self.w], self.src[:, bass.ds(n * (2 * self.w) + r * self.w, self.w)]
                         ).then_inc(self.kit.w_landed[r].sem, 16)

    def cut(self, pool, n):
        for r in range(2):
            raw = self.kit.raw[r][:, 0:self.w]
            at = bass.ds(n * (2 * self.w) + (self.to + r * self.w), self.w)
            pool.wait_ge(self.kit.w_landed[r].sem, self.kit.w_landed[r].at(n, 1))
            pool.tensor_copy(self.kit.w_hi[:, at], raw).then_inc(self.kit.w_split.sem, 1)
            pool.wait_ge(self.kit.w_split.sem, self.kit.w_split.at(n, 2 * r + 1))
            pool.tensor_tensor(self.kit.w_lo[:, at], raw, self.kit.w_hi[:, at].bitcast(F32),
                               ALU.subtract).then_inc(self.kit.w_split.sem, 1)

    def cut_high(self, act, n):
        for r in range(2):
            at = bass.ds(n * (2 * self.w) + (self.to + r * self.w), self.w)
            act.wait_ge(self.kit.w_landed[r].sem, self.kit.w_landed[r].at(n, 1))
            act.wait_ge(self.kit.w_split.sem, self.kit.w_split.at(n, 2 * r))
            act.activation(self.kit.w_hi[:, at], self.kit.raw[r][:, 0:self.w], ACT.Identity
                           ).then_inc(self.kit.w_split.sem, 1)

    def cut_low(self, pool, n):
        for r in range(2):
            at = bass.ds(n * (2 * self.w) + (self.to + r * self.w), self.w)
            pool.wait_ge(self.kit.w_split.sem, self.kit.w_split.at(n, 2 * r + 1))
            pool.tensor_tensor(self.kit.w_lo[:, at], self.kit.raw[r][:, 0:self.w], self.kit.w_hi[:, at].bitcast(F32),
                               ALU.subtract).then_inc(self.kit.w_split.sem, 1)

    def end(self):
        self.kit.w_split.end(self.passes)
        for landed in self.kit.w_landed:
            landed.end(self.passes)


SIGNALS = ("taken w_split set_up set_up_v varied rooted normed flipped shaped cut projected q_high qk_cut v_made scored "
           "maxed top_high top_cut shifted exped masked_off0 masked_off1 weighed mended mended_part quot_high sent stored "
           "up bent hid_cut down summed varied_again rooted_again regained gated grown "
           "planted judged valued walked veiled turned_out leaf_high leaf_low gathered landed_y").split()
DMA_SIGNALS = ("w_landed0 w_landed1 rows_in x_in ctx_in const_in parked0 parked1 stacked0 stacked1 topped").split()


class Kit:

    def __init__(self, nc, ctx, dram):
        self.nc, self.dram = nc, dram
        self.counters = {n: Signal(ctx.enter_context(nc.semaphore(n))) for n in SIGNALS}
        self.counters.update({n: DmaSignal(ctx.enter_context(nc.semaphore(n))) for n in DMA_SIGNALS})
        start = (nc.sbuf_base + 127) // 128 * 128
        end = nc.sbuf_usable_end // 32 * 32
        at = start
        self.w_hi = nc.alloc_sbuf_tensor_at("w_hi", [P, 3 * SLOT], F32R, offset=at)
        self.w_lo = nc.alloc_sbuf_tensor_at("w_lo", [P, 3 * SLOT], F32R, offset=at + 12 * SLOT)
        self.slot_ranges = [[(at + 4 * SLOT * k, at + 4 * SLOT * (k + 1)),
                             (at + 4 * SLOT * (k + 3), at + 4 * SLOT * (k + 4))] for k in range(3)]
        at += 24 * SLOT
        self.raw = [nc.alloc_sbuf_tensor_at(f"raw{r}", [P, PIECE], F32, offset=at + 4 * PIECE * r) for r in range(2)]
        at += 8 * PIECE
        self.x = nc.alloc_sbuf_tensor_at("x", [P, NT, C], F32, offset=at)
        self.x_range = (at, at + 4 * NT * C)
        at += 4 * NT * C
        self.ctx_n = nc.alloc_sbuf_tensor_at("ctx_n", [P, NT, CD], F32, offset=at)
        self.ctx_t = nc.alloc_sbuf_tensor_at("ctx_t", [P, B * S], F32, offset=at)
        at += 4 * NT * CD
        fixed = Space(nc, "all", [(at, at + 4 * KIB)])
        self.ident = fixed.take("ident", [P, P])
        self.tri = fixed.take("tri", [P, 2, P])
        self.cols = fixed.take("cols", [P, dram["cols"].shape[1]])
        self.power = fixed.take("power", [P, NT])
        self.pick = fixed.take("pick", [P, P], F32R)
        self.lower = fixed.take("lower", [P, E, E])
        at += 4 * KIB
        self.x1 = nc.alloc_sbuf_tensor_at("x1", [P, NT, C], F32, offset=at)
        self.xo = nc.alloc_sbuf_tensor_at("xo", [P, NT, C], F32, offset=at + 4 * NT * C)
        self.late = [(at, end)]
        self.early = [(at + 8 * NT * C, end), self.x_range]
        self.w_split = self.counter("w_split")
        self.w_landed = [self.counter(f"w_landed{r}") for r in range(2)]

    def counter(self, name):
        return self.counters[name]

    def apart(self, engine):
        engine.sem_inc(self.counter("taken").sem, 1)

    def weights(self, at, n, rows=P):
        return self.w_hi[0:rows, at:at + n], self.w_lo[0:rows, at:at + n]

    def column(self, name, k=0, rows=P):
        at = self.dram["col_at"][name] + k
        return self.cols[0:rows, at:at + 1]


def attention(kit, tag, heads_d, masked, kv, scale, own, pre, affine=None, ctx_affine=None,
              q_bias=None, k_bias=None, v_bias=None, out_bias=None, free=()):
    nc, dram = kit.nc, kit.dram
    d = heads_d
    mt = HH * d // P
    kvt = CT if kv == "self" else 1
    in_x = kit.x if kv == "raw" else kit.x1
    qn, kn = CT * HEADS * d, kvt * HEADS * d
    w_q, w_k, w_v, w_o = own, own + qn, own + qn + kn, own + qn + 2 * kn

    with ExitStack() as ctx:
        work = Space(nc, tag, [*free, *(kit.late if kv == "raw" else kit.early)])
        stack_q = [work.take(f"stack_q{h}", [98, HH, S], F32R) for h in range(2)]
        stack_k = [work.take(f"stack_k{h}", [98, HH, S], F32R) for h in range(2)]
        n_in = work.take("n_in", [P, TB, C])
        q_in = [work.take(f"q_in_{p}", [P, CT, S], F32R) for p in ("hi", "lo")]
        kv_in = q_in
        if kv != "self" or ctx_affine:
            kv_in = [work.take(f"kv_in_{p}", [P, kvt, S], F32R) for p in ("hi", "lo")]
        ctx_now = work.take("ctx_now", [P, TB, CD]) if kv == "norm" else None
        turned = work.take("turned", [P, CT, S]) if affine else None
        turned_kv = work.take("turned_kv", [P, kvt, S]) if affine else None
        qk = work.take("qk", [P, 4, mt, S], F32R)
        v = [work.take(f"v{h}", [P, TB, HH, 32]) for h in range(2)]
        probs = [work.take(f"probs{s}", [P, 2, TB, S]) for s in range(2)]
        kept = [work.take(f"kept{s}", [P, 2, TB, P]) for s in range(2)] if masked else None
        o_hi = work.take("o_hi", [P, HEADS // 4, S], F32R)
        o_lo = work.take("o_lo", [P, HEADS // 4, S], F32R)
        o_one = [work.take(f"o_one{g}", [P, S]) for g in range(2)]
        top = work.take("top", [P, TB, HH])
        top_hi = work.take("top_hi", [HH, S], F32R)
        top_lo = work.take("top_lo", [HH, S], F32R)
        stats = work.take("stats", [P, TB, 6])
        mean_var = work.take("mean_var", [P, TB, 2])
        spread = work.take("spread", [P, TB, 1])
        rstd = work.take("rstd", [P, TB, 1])
        ones = work.take("ones", [P, 32])
        rows = {}
        for name in (out_bias, v_bias):
            if name:
                rows[name] = work.take(name, [P, C])

        ps_score = [ctx.enter_context(nc.psum_tensor(f"{tag}_ps_score{s}", [P, 4, S], F32)) for s in range(2)]
        ps_out = [ctx.enter_context(nc.psum_tensor(f"{tag}_ps_out{g}", [P, 2, S], F32)) for g in range(2)]
        ps_front = [ctx.enter_context(nc.psum_tensor(f"{tag}_ps_front{g}", [P, 2 * S], F32)) for g in range(2)]

        set_up = kit.counter("set_up")
        set_up_v = kit.counter("set_up_v")
        rows_in = kit.counter("rows_in")
        varied = kit.counter("varied")
        rooted = kit.counter("rooted")
        normed = kit.counter("normed")
        flipped = kit.counter("flipped")
        shaped = kit.counter("shaped")
        cut = kit.counter("cut")
        projected = kit.counter("projected")
        q_high = kit.counter("q_high")
        qk_cut = kit.counter("qk_cut")
        v_made = kit.counter("v_made")
        parked = [kit.counter(f"parked{n}") for n in range(2)]
        stacked = [kit.counter(f"stacked{h}") for h in range(2)]
        scored = kit.counter("scored")
        maxed = kit.counter("maxed")
        top_high = kit.counter("top_high")
        top_cut = kit.counter("top_cut")
        topped = kit.counter("topped")
        shifted = kit.counter("shifted")
        exped = kit.counter("exped")
        masked_off = [kit.counter(f"masked_off{n}") for n in range(2)]
        weighed = kit.counter("weighed")
        mended = kit.counter("mended")
        mended_part = kit.counter("mended_part")
        quot_high = kit.counter("quot_high")
        sent = kit.counter("sent")
        stored = kit.counter("stored")

        set_up.begin(5 if d < 32 else 1)
        set_up_v.begin(4 if d < 32 else 2)
        rows_in.begin(len(rows))
        varied.begin(1 + 2)
        rooted.begin(1)
        normed.begin(1)
        flipped.begin(2 if kv == "norm" else 1)
        shaped.begin(2)
        cut.begin(2)
        projected.begin(6)
        q_high.begin(4)
        qk_cut.begin(4)
        v_made.begin(2)
        for s_ in parked:
            s_.begin(2)
        for s_ in stacked:
            s_.begin(6)
        scored.begin(10)
        maxed.begin(8)
        top_high.begin(2)
        top_cut.begin(2)
        topped.begin(4)
        shifted.begin(8)
        exped.begin(8)
        for s_ in masked_off:
            s_.begin(4)
        weighed.begin(8)
        mended.begin(4)
        mended_part.begin(2 * 4)
        quot_high.begin(4)
        sent.begin(1)
        stored.begin(1 + (1 if out_bias else 0))
        fetch = Prefetch(kit, *pre, B)

        block = ctx.enter_context(nc.Block())

        def mask_two(engine, b, h, k):
            if masked:
                engine.wait_ge(exped.sem, exped.at(b, 4 * h + k + 1))
                engine.wait_ge(weighed.sem, weighed.at(b, 4 * h + k - 1))
                for t in range(TB):
                    last = engine.tensor_tensor(kept[k % 2][:, :, t, :], probs[k % 2][:, :, t, t * P:(t + 1) * P],
                                                kit.tri[:, :, :], ALU.mult)
                last.then_inc(masked_off[k % 2].sem, 1)

        @block.sync
        def _(sp):
            for n, name in enumerate(rows):
                sp.dma_start(rows[name][:, :], dram["rows"][name].broadcast_to([P, C])).then_inc(rows_in.sem, 16)

            def park(b, h, n):
                comps = slice(2 - 2 * n, 4 - 2 * n)
                sp.wait_ge(qk_cut.sem, qk_cut.at(b, 2 * h + n + 1))
                if n == 0:
                    sp.wait_ge(stacked[h].sem, stacked[h].at(b, 0))
                sp.dma_start(dram["heads"][h, comps, 0:HH * d, :].rearrange("c (m p) q -> p c m q", p=P),
                             qk[:, comps, :, :].bitcast(F32)).then_inc(parked[n].sem, 16)

            def stack(b, h):
                for n, (to, order) in enumerate(((stack_k[h], (2, 3, 2)), (stack_q[h], (0, 0, 1)))):
                    sp.wait_ge(parked[n].sem, parked[n].at(b, h + 1))
                    if n == 0:
                        kit.apart(sp)
                        sp.wait_ge(shifted.sem, shifted.at(b, 4 * h - 4))
                    for at, comp in enumerate(order):
                        sp.dma_start(to[32 * at:32 * at + d, :, :].bitcast(F32),
                                     dram["heads"][h, comp, 0:HH * d, :].rearrange("(h d) q -> d h q", d=d)
                                     ).then_inc(stacked[h].sem, 16)

            def crown(b, h):
                sp.wait_ge(top_cut.sem, top_cut.at(b, h + 1))
                sp.dma_start(stack_q[h][96:97, :, :].bitcast(F32), top_hi[:, :].bitcast(F32)).then_inc(topped.sem, 16)
                sp.dma_start(stack_q[h][97:98, :, :].bitcast(F32), top_lo[:, :].bitcast(F32)).then_inc(topped.sem, 16)

            def body(b, last):
                fetch.load(sp, b)
                if not last:
                    park(b + 1, 0, 0)
                crown(b, 1)
                if not last:
                    park(b + 1, 0, 1)
                    stack(b + 1, 0)
                    park(b + 1, 1, 0)
                    crown(b + 1, 0)
                    park(b + 1, 1, 1)
                    stack(b + 1, 1)

            park(0, 0, 0)
            park(0, 0, 1)
            if d < 32:
                sp.wait_ge(set_up.sem, set_up.at(0, 5))
            stack(0, 0)
            park(0, 1, 0)
            crown(0, 0)
            park(0, 1, 1)
            stack(0, 1)
            with sp.Fori(0, B - 1) as b:
                body(b, False)
            body(B - 1, True)

        @block.gpsimd
        def _(pool):
            def root(b):
                pool.wait_ge(varied.sem, varied.at(b, 3))
                pool.tensor_tensor(rstd[:, :, 0], spread[:, :, 0], kit.power[:, 0:TB], ALU.pow).then_inc(rooted.sem, 1)

            root(0)
            pool.memset(ones[:, :], 1.0).then_inc(set_up.sem, 1)
            if d < 32:
                for to in (*stack_k, *stack_q):
                    pool.memset(to[0:96, :, :].bitcast(F32), 0.0).then_inc(set_up.sem, 1)

            def mask(b, h):
                mask_two(pool, b, h, 0)
                mask_two(pool, b, h, 2)

            def body(b, last):
                if not last:
                    root(b + 1)
                mask(b, 0)
                fetch.cut(pool, b)
                mask(b, 1)

            with pool.Fori(0, B - 1) as b:
                body(b, False)
            body(B - 1, True)

        @block.scalar
        def _(act):
            def flip_out(b):
                act.wait_ge(flipped.sem, flipped.at(b, 1))
                for t in range(kvt):
                    if kv == "raw":
                        last = act.activation(kv_in[0][:, t, :], kit.ctx_t[:, bass.ds(b * S, S)], ACT.Identity)
                        continue
                    got = ps_front[0 if kv == "norm" else 1][:, t * S:(t + 1) * S]
                    put = {"bias": kit.column(ctx_affine[1], t), "scale": kit.column(ctx_affine[0], t)}
                    act.activation(turned_kv[:, t, :], got, ACT.Identity, **put)
                    last = act.activation(kv_in[0][:, t, :], got, ACT.Identity, **put)
                last.then_inc(shaped.sem, 1)
                act.wait_ge(flipped.sem, flipped.at(b, flipped.per))
                for t in range(CT):
                    got = ps_front[1][:, t * S:(t + 1) * S]
                    if affine:
                        put = {"bias": kit.column(affine[1], t), "scale": kit.column(affine[0], t)}
                        act.activation(turned[:, t, :], got, ACT.Identity, **put)
                        last = act.activation(q_in[0][:, t, :], got, ACT.Identity, **put)
                    else:
                        last = act.activation(q_in[0][:, t, :], got, ACT.Identity)
                last.then_inc(shaped.sem, 1)

            def high(b, h, ns=(0, 1)):
                for n in ns:
                    k = 1 - n
                    act.wait_ge(projected.sem, projected.at(b, 3 * h + n + 1))
                    act.wait_ge(parked[n].sem, parked[n].at(b, h))
                    bias = (q_bias, k_bias)[k]
                    for m in range(mt):
                        last = act.activation(qk[:, 2 * k, m, :], ps_front[1 - k][:, m * S:(m + 1) * S], ACT.Identity,
                                              bias=kit.column(bias, h * mt + m) if bias else 0.0)
                    last.then_inc(q_high.sem, 1)

            def crown(b, h):
                act.wait_ge(scored.sem, scored.at(b, 5 * h + 5))
                act.wait_ge(topped.sem, topped.at(b, 2 * h))
                act.activation(top_hi[:, :], ps_front[1][0:HH, 0:S], ACT.Identity, scale=-1.0).then_inc(top_high.sem, 1)

            def exp(b, h, k):
                act.wait_ge(shifted.sem, shifted.at(b, 4 * h + k + 1))
                act.wait_ge(weighed.sem, weighed.at(b, 4 * h + k - 1))
                act.activation(probs[k % 2][:, :, :, :].rearrange("p h t q -> p (h t q)"),
                               ps_score[k % 2][:, :, :].rearrange("p a q -> p (a q)"), ACT.Exp,
                               scale=scale).then_inc(exped.sem, 1)

            def quotients(b, n):
                act.wait_ge(mended_part.sem, mended_part.at(b, 2 * n + 2))
                act.activation(o_hi[:, n % 4, :], o_one[n % 2][:, :], ACT.Identity).then_inc(quot_high.sem, 1)

            def body(b, first, last):
                exp(b, 0, 0)
                exp(b, 0, 1)
                if not first:
                    quotients(b, -1)
                exp(b, 0, 2)
                if not last:
                    flip_out(b + 1)
                exp(b, 0, 3)
                if not last:
                    high(b + 1, 0, (0,))
                crown(b, 1)
                if not last:
                    high(b + 1, 0, (1,))
                quotients(b, 0)
                exp(b, 1, 0)
                exp(b, 1, 1)
                quotients(b, 1)
                exp(b, 1, 2)
                exp(b, 1, 3)
                if not last:
                    high(b + 1, 1, (0,))
                    crown(b + 1, 0)
                    high(b + 1, 1, (1,))
                quotients(b, 2)

            flip_out(0)
            high(0, 0)
            high(0, 1, (0,))
            crown(0, 0)
            high(0, 1, (1,))
            body(0, True, False)
            with act.Fori(1, B - 1) as b:
                body(b, False, False)
            body(B - 1, False, True)
            quotients(B, -1)

        @block.vector
        def _(dve):
            for h in range(2):
                if d < 32:
                    dve.memset(v[h][:, :, :, :], 0.0).then_inc(set_up_v.sem, 1)
                dve.memset(stack_k[h][96:98, :, :].bitcast(F32), 1.0).then_inc(set_up_v.sem, 1)

            def vary(b):
                for i in range(TB):
                    tile = in_x[:, b * TB + i, :]
                    last = dve.bn_stats(stats[:, i, :], tile)
                last.then_inc(varied.sem, 1)
                dve.wait_ge(varied.sem, varied.at(b, 1))
                kit.apart(dve)
                for i in range(TB):
                    last = dve.bn_aggr(mean_var[:, i, :], stats[:, i, :])
                last.then_inc(varied.sem, 1)
                dve.wait_ge(varied.sem, varied.at(b, 2))
                dve.tensor_scalar(spread[:, :, :], mean_var[:, :, 1:2], EPS, None, ALU.add).then_inc(varied.sem, 1)

            def norm(b):
                dve.wait_ge(rooted.sem, rooted.at(b, 1))
                dve.wait_ge(flipped.sem, flipped.at(b, 0))
                for i in range(TB):
                    last = dve.tensor_scalar(n_in[:, i, :], in_x[:, b * TB + i, :], mean_var[:, i, 0:1], rstd[:, i, :],
                                             ALU.subtract, ALU.mult)
                if kv == "norm":
                    last = dve.tensor_copy(ctx_now[:, :, :], kit.ctx_n[:, bass.ds(b * TB, TB), :])
                last.then_inc(normed.sem, 1)

            def flip_out(b):
                pairs = [(kv_in, turned_kv if affine else kit.ctx_t, kvt),
                         (q_in, turned if affine else ps_front[1], CT)]
                for n, (to, full, width) in enumerate(pairs):
                    dve.wait_ge(shaped.sem, shaped.at(b, n + 1))
                    hi, lo = (x[:, :, :].rearrange("p t q -> p (t q)") for x in to)
                    if affine:
                        src = full[:, :, :].rearrange("p t q -> p (t q)")
                    else:
                        src = full[:, :] if n else full[:, bass.ds(b * S, S)]
                    dve.tensor_tensor(lo, src, hi.bitcast(F32), ALU.subtract).then_inc(cut.sem, 1)

            def low(b, h, ns=(0, 1)):
                for n in ns:
                    k = 1 - n
                    dve.wait_ge(q_high.sem, q_high.at(b, 2 * h + n + 1))
                    bias = (q_bias, k_bias)[k]
                    for m in range(mt):
                        src = ps_front[1 - k][:, m * S:(m + 1) * S]
                        if bias:
                            last = dve.scalar_tensor_tensor(qk[:, 2 * k + 1, m, :], src, kit.column(bias, h * mt + m),
                                                            qk[:, 2 * k, m, :].bitcast(F32), ALU.add, ALU.subtract)
                        else:
                            last = dve.tensor_tensor(qk[:, 2 * k + 1, m, :], src, qk[:, 2 * k, m, :].bitcast(F32),
                                                     ALU.subtract)
                    last.then_inc(qk_cut.sem, 1)

            def make_v(b, h):
                dve.wait_ge(projected.sem, projected.at(b, 3 * h + 3))
                for i in range(TB):
                    src = ps_front[1][:, i * HH * d:(i + 1) * HH * d].rearrange("p (h d) -> p h d", d=d)
                    if v_bias:
                        last = dve.tensor_tensor(v[h][:, i, :, 0:d], src, rows[v_bias][:, h * HH * d:(h + 1) * HH * d]
                                                 .rearrange("p (h d) -> p h d", d=d), ALU.add)
                    else:
                        last = dve.tensor_copy(v[h][:, i, :, 0:d], src)
                last.then_inc(v_made.sem, 1)

            def tops(b, h):
                for k in range(4):
                    i, g = k // 2, k % 2
                    dve.wait_ge(scored.sem, scored.at(b, 5 * h + k + 1))
                    dve.tensor_reduce(top[:, i, 4 * g:4 * g + 4], ps_score[k % 2][:, :, :], AX.X, ALU.max
                                      ).then_inc(maxed.sem, 1)

            def split_tops(b, h):
                dve.wait_ge(top_high.sem, top_high.at(b, h + 1))
                dve.scalar_tensor_tensor(top_lo[:, :], ps_front[1][0:HH, 0:S], -1.0, top_hi[:, :].bitcast(F32),
                                         ALU.mult, ALU.subtract).then_inc(top_cut.sem, 1)

            def divide(b, n):
                one, got = o_one[n % 2][:, :], ps_out[n % 2]
                dve.wait_ge(weighed.sem, weighed.at(b, 2 * n + 2))
                dve.wait_ge(mended.sem, mended.at(b, n - 1))
                dve.reciprocal(one, got[:, 1, :]).then_inc(mended_part.sem, 1)
                dve.wait_ge(mended_part.sem, mended_part.at(b, 2 * n + 1))
                dve.tensor_tensor(one, got[:, 0, :], one, ALU.mult).then_inc(mended_part.sem, 1)

            def mend(b, n):
                for n in (n, n + 1):
                    dve.wait_ge(quot_high.sem, quot_high.at(b, n + 1))
                    dve.tensor_tensor(o_lo[:, n % 4, :], o_one[n % 2][:, :], o_hi[:, n % 4, :].bitcast(F32),
                                      ALU.subtract).then_inc(mended.sem, 1)

            def store(b):
                dve.wait_ge(sent.sem, sent.at(b, 1))
                got = ps_front[0][:, :].rearrange("p (i c) -> p i c", c=C)
                tiles = bass.ds(b * TB, TB)
                to = kit.x if kv == "raw" else kit.xo
                if out_bias:
                    dve.tensor_tensor(to[:, tiles, :], got, in_x[:, tiles, :], ALU.add).then_inc(stored.sem, 1)
                    dve.wait_ge(stored.sem, stored.at(b, 1))
                    for i in range(TB):
                        last = dve.tensor_tensor(to[:, b * TB + i, :], to[:, b * TB + i, :], rows[out_bias][:, :], ALU.add)
                    last.then_inc(stored.sem, 1)
                else:
                    dve.tensor_tensor(to[:, tiles, :], got, in_x[:, tiles, :], ALU.add).then_inc(stored.sem, 1)

            def body(b, first, last):
                if not last:
                    vary(b + 1)
                if not first:
                    divide(b, -1)
                make_v(b, 1)
                mask_two(dve, b, 0, 1)
                if not last:
                    norm(b + 1)
                if not first:
                    mend(b, -2)
                if not last:
                    flip_out(b + 1)
                mask_two(dve, b, 0, 3)
                if not first:
                    store(b - 1)
                tops(b, 1)
                if not last:
                    low(b + 1, 0, (0,))
                split_tops(b, 1)
                divide(b, 0)
                if not last:
                    low(b + 1, 0, (1,))
                divide(b, 1)
                if not last:
                    make_v(b + 1, 0)
                mask_two(dve, b, 1, 1)
                mend(b, 0)
                mask_two(dve, b, 1, 3)
                if not last:
                    tops(b + 1, 0)
                    low(b + 1, 1, (0,))
                    split_tops(b + 1, 0)
                divide(b, 2)
                if not last:
                    low(b + 1, 1, (1,))

            if rows:
                dve.wait_ge(rows_in.sem, rows_in.at(0, len(rows)))
            dve.wait_ge(set_up_v.sem, set_up_v.at(0, set_up_v.per))
            vary(0)
            norm(0)
            flip_out(0)
            low(0, 0)
            make_v(0, 0)
            tops(0, 0)
            low(0, 1, (0,))
            split_tops(0, 0)
            low(0, 1, (1,))
            body(0, True, False)
            with dve.Fori(1, B - 1) as b:
                body(b, False, False)
            body(B - 1, False, True)
            divide(B, -1)
            mend(B, -2)
            store(B - 1)

        @block.tensor
        def _(pe):
            pe.wait_ge(set_up.sem, set_up.at(0, 1))
            pe.wait_ge(set_up_v.sem, set_up_v.at(0, set_up_v.per))

            def flip(b):
                pe.wait_ge(normed.sem, normed.at(b, 1))
                if kv == "norm":
                    pe.wait_ge(qk_cut.sem, qk_cut.at(b, -1))
                    for i in range(TB):
                        last = pe.transpose(ps_front[0][:, i * P:(i + 1) * P], ctx_now[:, i, :], kit.ident[:, :])
                    last.then_inc(flipped.sem, 1)
                pe.wait_ge(v_made.sem, v_made.at(b, 0))
                for t in range(CT):
                    for i in range(TB):
                        last = pe.transpose(ps_front[1][:, t * S + i * P:t * S + (i + 1) * P],
                                            n_in[:, i, t * P:(t + 1) * P], kit.ident[:, :])
                last.then_inc(flipped.sem, 1)

            def project_k(b, h, ms):
                pe.wait_ge(cut.sem, cut.at(b, 1))
                pe.wait_ge(qk_cut.sem, qk_cut.at(b, 1 if h else -1))
                pe.wait_ge(stored.sem, stored.at(b, -stored.per))
                for m in ms:
                    at = w_k + (h * mt + m) * P
                    for t in range(kvt):
                        last = product(pe, ps_front[0][:, m * S:(m + 1) * S],
                                       kit.weights(at + t * HEADS * d, P),
                                       [x[:, t, :] for x in kv_in], t == 0, t == kvt - 1)
                if mt - 1 in ms:
                    last.then_inc(projected.sem, 1)

            def project_q(b, h):
                pe.wait_ge(cut.sem, cut.at(b, 2))
                pe.wait_ge(top_cut.sem, top_cut.at(b, h))
                for m in range(mt):
                    at = w_q + (h * mt + m) * P
                    for t in range(CT):
                        last = product(pe, ps_front[1][:, m * S:(m + 1) * S],
                                       kit.weights(at + t * HEADS * d, P),
                                       [x[:, t, :] for x in q_in], t == 0, t == CT - 1)
                last.then_inc(projected.sem, 1)

            def project_v(b, h):
                pe.wait_ge(qk_cut.sem, qk_cut.at(b, 2 * h + 2))
                for i in range(TB):
                    at = w_v + h * HH * d
                    for t in range(kvt):
                        last = product(pe, ps_front[1][:, i * HH * d:(i + 1) * HH * d],
                                       [x[:, t, i * P:(i + 1) * P] for x in kv_in],
                                       kit.weights(at + t * HEADS * d, HH * d), t == 0, t == kvt - 1)
                last.then_inc(projected.sem, 1)

            def score(b, h, ks):
                pe.wait_ge(stacked[h].sem, stacked[h].at(b, 6))
                for k in ks:
                    i, g = k // 2, k % 2
                    if k < 2:
                        pe.wait_ge(exped.sem, exped.at(b, 4 * h - 1 + k))
                    else:
                        pe.wait_ge(maxed.sem, maxed.at(b, 4 * h + k - 1))
                    for j in range(4):
                        last = pe.matmul(ps_score[k % 2][:, j, :], stack_q[h][0:96, 4 * g + j, i * P:(i + 1) * P],
                                         stack_k[h][0:96, 4 * g + j, :], start=True, stop=True)
                    last.then_inc(scored.sem, 1)

            def turn_tops(b, h, last_pass):
                pe.wait_ge(maxed.sem, maxed.at(b, 4 * h + 4))
                pe.wait_ge(v_made.sem, v_made.at(b, h + 1))
                if h and not last_pass:
                    pe.wait_ge(cut.sem, cut.at(b, 4))
                for i in range(TB):
                    last = pe.transpose(ps_front[1][0:HH, i * P:(i + 1) * P], top[:, i, :], kit.ident[:, :])
                last.then_inc(scored.sem, 1)

            def shift(b, h, k):
                if k >= 2:
                    pe.wait_ge(exped.sem, exped.at(b, 4 * h + k - 1))
                for j in range(2):
                    for t in range(TB):
                        last = pe.matmul(ps_score[k % 2][:, 2 * j + t, :], stack_k[h][0:98, 2 * k + j, t * P:(t + 1) * P],
                                         stack_q[h][0:98, 2 * k + j, :], start=True, stop=True)
                last.then_inc(shifted.sem, 1)

            def weigh(b, h, k):
                g = k // 2
                if k % 2 == 0:
                    pe.wait_ge(mended_part.sem, mended_part.at(b, 4 * h + 2 * g - 2))
                pe.wait_ge(exped.sem, exped.at(b, 4 * h + k + 1))
                if masked:
                    pe.wait_ge(masked_off[k % 2].sem, masked_off[k % 2].at(b, 2 * h + k // 2 + 1))
                for j in range(2):
                    r = 32 * (2 * (k % 2) + j)
                    p = probs[k % 2]
                    vh = [v[h][:, t, 2 * k + j, :] for t in range(TB)]
                    o = ps_out[g][r:r + 32, 0, :]
                    if masked:
                        m = kept[k % 2]
                        pe.matmul(o[:, 0:P], vh[0], m[:, j, 0, :], start=True, stop=False, tile_position=(0, r))
                        pe.matmul(o[:, 0:P], vh[1], p[:, j, 1, 0:P], start=False, stop=True, tile_position=(0, r))
                        pe.matmul(o[:, P:S], vh[1], m[:, j, 1, :], start=True, stop=True, tile_position=(0, r))
                    else:
                        for t in range(TB):
                            pe.matmul(o, vh[t], p[:, j, t, :], start=t == 0, stop=t == TB - 1, tile_position=(0, r))
                    for t in range(TB):
                        last = pe.matmul(ps_out[g][r:r + 32, 1, :], ones[:, :], p[:, j, t, :], start=t == 0,
                                         stop=t == TB - 1, tile_position=(0, r))
                last.then_inc(weighed.sem, 1)

            def send(b):
                pe.wait_ge(mended.sem, mended.at(b, 4))
                pe.wait_ge(qk_cut.sem, qk_cut.at(b, 3))
                pe.wait_ge(stored.sem, stored.at(b, 0))
                for i in range(TB):
                    for t in range(HEADS // 4):
                        done = product(pe, ps_front[0][:, i * C:(i + 1) * C],
                                       [x[:, t, i * P:(i + 1) * P] for x in (o_hi, o_lo)],
                                       kit.weights(w_o + t * C, C), t == 0, t == HEADS // 4 - 1)
                done.then_inc(sent.sem, 1)

            def attend(b, h, first, last):
                pe.wait_ge(topped.sem, topped.at(b, 2 * h + 2))
                after = (b, 1) if h == 0 else (b + 1, 0)
                more = h == 0 or not last
                shift(b, h, 0)
                shift(b, h, 1)
                if more:
                    project_v(*after)
                weigh(b, h, 0)
                shift(b, h, 2)
                weigh(b, h, 1)
                if h == 0 and not last:
                    flip(b + 1)
                shift(b, h, 3)
                weigh(b, h, 2)
                if h == 0 and not first:
                    if kv == "norm" and not last:
                        pe.wait_ge(shaped.sem, shaped.at(b, 3))
                    pe.wait_ge(qk_cut.sem, qk_cut.at(b, 3))
                    send(b - 1)
                if more:
                    score(*after, (0, 1))
                weigh(b, h, 3)
                early = mt // 2 if kvt == CT else 0
                if not last and early:
                    project_k(b + 1, h, range(early))
                if more:
                    score(*after, (2, 3))
                if not last:
                    project_k(b + 1, h, range(early, mt))
                if more:
                    turn_tops(*after, last)
                if not last:
                    project_q(b + 1, h)

            def body(b, first, last):
                attend(b, 0, first, last)
                attend(b, 1, first, last)

            flip(0)
            project_k(0, 0, range(mt))
            project_q(0, 0)
            project_v(0, 0)
            score(0, 0, (0, 1, 2, 3))
            project_k(0, 1, range(mt))
            turn_tops(0, 0, False)
            project_q(0, 1)
            body(0, True, False)
            with pe.Fori(1, B - 1) as b:
                body(b, False, False)
            body(B - 1, False, True)
            send(B - 1)

    fetch.end()
    for s_ in (set_up, set_up_v, rows_in):
        s_.end(1)
    for s_ in (varied, rooted, normed, flipped, shaped, cut, projected, q_high, qk_cut, v_made, *parked, *stacked, scored,
               maxed, top_high, top_cut, topped, shifted, exped, *(masked_off if masked else ()), weighed, mended,
               mended_part, quot_high, sent, stored):
        s_.end(B)


def opening(kit):
    nc, dram = kit.nc, kit.dram
    weight_passes = 4
    with ExitStack():
        work = Space(nc, "open", [kit.slot_ranges[1][0], kit.slot_ranges[1][1]])
        gain = work.take("gain", [P, C])
        offset = work.take("offset", [P, C])
        stats = work.take("stats", [P, NT, 6])
        mean_var = work.take("mean_var", [P, NT, 2])
        spread = work.take("spread", [P, NT])
        rstd = work.take("rstd", [P, NT])
        x_in, const_in, ctx_in = (kit.counter(n) for n in ("x_in", "const_in", "ctx_in"))
        varied, rooted = kit.counter("varied"), kit.counter("rooted")
        powered = kit.counter("set_up")
        for s in (x_in, ctx_in):
            s.begin(1)
        const_in.begin(6)
        varied.begin(5)
        rooted.begin(1)
        powered.begin(3)
        fetch = Prefetch(kit, dram["w_a1"], 0, SLOT, weight_passes)
        with nc.Block() as block:

            @block.sync
            def _(sp):
                sp.dma_start(kit.x[:, :, :], dram["x"]).then_inc(x_in.sem, 16)
                fetch.load(sp, 0)
                sp.dma_start(gain[:, :], dram["rows"]["ln1_g"].broadcast_to([P, C])).then_inc(const_in.sem, 16)
                sp.dma_start(offset[:, :], dram["rows"]["ln1_b"].broadcast_to([P, C])).then_inc(const_in.sem, 16)
                sp.dma_start(kit.ctx_n[:, :, :], dram["ctx"]).then_inc(ctx_in.sem, 16)
                sp.dma_start(kit.ident[:, :], dram["ident"]).then_inc(const_in.sem, 16)
                sp.dma_start(kit.tri[:, :, :], dram["tri"]).then_inc(const_in.sem, 16)
                sp.dma_start(kit.cols[:, :], dram["cols"]).then_inc(const_in.sem, 16)
                sp.dma_start(kit.lower[:, :, :], dram["lower"]).then_inc(const_in.sem, 16)
                for n in range(1, weight_passes):
                    fetch.load(sp, n)

            @block.gpsimd
            def _(pool):
                for s in kit.counters.values():
                    pool.sem_inc(s.sem, s.CREDIT)
                pool.memset(kit.power[:, :], -0.5).then_inc(powered.sem, 1)
                pool.memset(kit.pick[:, :].bitcast(F32), 0.0).then_inc(powered.sem, 1)
                pool.wait_ge(powered.sem, powered.at(0, 2))
                pool.memset(kit.pick[0:2, :].bitcast(F32), 1.0).then_inc(powered.sem, 1)
                fetch.cut_low(pool, 0)
                for n in range(3):
                    pool.wait_ge(varied.sem, varied.at(n, 3))
                    pool.tensor_tensor(rstd[:, :], spread[:, :], kit.power[:, :], ALU.pow).then_inc(rooted.sem, 1)
                for n in range(1, weight_passes):
                    fetch.cut_low(pool, n)

            @block.scalar
            def _(act):
                for n in range(weight_passes):
                    fetch.cut_high(act, n)

            @block.vector
            def _(dve):
                def normalise(n, src, to):
                    for t in range(NT):
                        last = dve.bn_stats(stats[:, t, :], src[:, t, :])
                    last.then_inc(varied.sem, 1)
                    dve.wait_ge(varied.sem, varied.at(n, 1))
                    kit.apart(dve)
                    for t in range(NT):
                        last = dve.bn_aggr(mean_var[:, t, :], stats[:, t, :])
                    last.then_inc(varied.sem, 1)
                    dve.wait_ge(varied.sem, varied.at(n, 2))
                    dve.tensor_scalar(spread[:, :], mean_var[:, :, 1], EPS, None, ALU.add).then_inc(varied.sem, 1)
                    dve.wait_ge(rooted.sem, rooted.at(n, 1))
                    for t in range(NT):
                        last = dve.tensor_scalar(to[:, t, :], src[:, t, :], mean_var[:, t, 0:1], rstd[:, t:t + 1],
                                                 ALU.subtract, ALU.mult)
                    last.then_inc(varied.sem, 1)
                    dve.wait_ge(varied.sem, varied.at(n, 4))

                dve.wait_ge(x_in.sem, x_in.at(0, 1))
                normalise(0, kit.x, kit.x1)
                dve.sem_inc(varied.sem, 1)
                normalise(1, kit.x1, kit.x1)
                dve.wait_ge(const_in.sem, const_in.at(0, 6))
                for t in range(NT):
                    last = dve.tensor_tensor(kit.x1[:, t, :], kit.x1[:, t, :], gain[:, :], ALU.mult)
                last.then_inc(varied.sem, 1)
                dve.wait_ge(varied.sem, varied.at(2, 0))
                for t in range(NT):
                    dve.tensor_tensor(kit.x1[:, t, :], kit.x1[:, t, :], offset[:, :], ALU.add)
                dve.wait_ge(ctx_in.sem, ctx_in.at(0, 1))
                normalise(2, kit.ctx_n, kit.ctx_n)
                dve.sem_inc(varied.sem, 1)
        fetch.end()
        for s in (x_in, ctx_in, const_in, powered):
            s.end(1)
        varied.end(3)
        rooted.end(3)


def feed_forward(kit, tag, own, pre, final, free=()):
    nc, dram = kit.nc, kit.dram
    w_up, w_down = own, own + CT * FF
    gain_, offset_, up_bias, down_bias = (f"{tag[1:]}_{n}" for n in ("ln3_g", "ln3_b", "li2_b", "li3_b"))
    row_names = [down_bias] if final else [down_bias, "ln2_g", "ln2_b"]

    with ExitStack() as ctx:
        work = Space(nc, tag, [*free, kit.early[0]])
        n_in = work.take("n_in", [P, CK, C])
        turned = work.take("turned", [P, CT, CHUNK])
        x_in = [work.take(f"x_{p}", [P, CT, CHUNK], F32R) for p in ("hi", "lo")]
        act_out = [work.take(f"act_out{s}", [P, CHUNK]) for s in range(2)]
        hid = [[work.take(f"hid_{p}{s}", [P, CHUNK], F32R) for p in ("hi", "lo")] for s in range(4)]
        stats = work.take("stats", [P, CK, 6])
        mean_var = work.take("mean_var", [P, CK, 2])
        spread = work.take("spread", [P, CK])
        rstd = work.take("rstd", [P, CK])
        rows = {name: work.take(name, [P, C]) for name in row_names}
        ps_y = [ctx.enter_context(nc.psum_tensor(f"{tag}_ps_y{i}", [P, 512], F32)) for i in range(CK)]
        ps_h = [ctx.enter_context(nc.psum_tensor(f"{tag}_ps_h{s}", [P, CHUNK], F32)) for s in range(2)]
        ps_t = [ctx.enter_context(nc.psum_tensor(f"{tag}_ps_t{t}", [P, CHUNK], F32)) for t in range(CT)]

        rows_in = kit.counter("rows_in")
        x_back = kit.counter("x_in")
        varied = kit.counter("varied")
        rooted = kit.counter("rooted")
        normed = kit.counter("normed")
        flipped = kit.counter("flipped")
        shaped = kit.counter("shaped")
        cut = kit.counter("cut")
        up = kit.counter("up")
        bent = kit.counter("bent")
        hid_cut = kit.counter("hid_cut")
        down = kit.counter("down")
        summed = kit.counter("summed")
        stored = kit.counter("stored")
        rows_in.begin(len(rows))
        x_back.begin(1)
        varied_again = kit.counter("varied_again")
        rooted_again = kit.counter("rooted_again")
        regained = kit.counter("regained")
        varied.begin(3)
        rooted.begin(1)
        varied_again.begin(3)
        rooted_again.begin(1)
        regained.begin(2)
        normed.begin(1)
        flipped.begin(1)
        shaped.begin(1)
        cut.begin(2)
        up.begin(FT)
        bent.begin(FT)
        hid_cut.begin(2 * FT)
        down.begin(FT)
        summed.begin(3 if final else 2)
        stored.begin(1)
        fetch = Prefetch(kit, *pre, NCH)
        block = ctx.enter_context(nc.Block())

        @block.sync
        def _(sp):
            for n, name in enumerate(rows):
                sp.dma_start(rows[name][:, :], dram["rows"][name].broadcast_to([P, C])).then_inc(rows_in.sem, 16)
            if final:
                sp.dma_start(kit.x[:, :, :], dram["x"]).then_inc(x_back.sem, 16)
            with sp.Fori(0, NCH) as c:
                fetch.load(sp, c)

        @block.gpsimd
        def _(pool):
            def root(c, seen, done):
                pool.wait_ge(seen.sem, seen.at(c, 3))
                pool.tensor_tensor(rstd[:, :], spread[:, :], kit.power[:, 0:CK], ALU.pow).then_inc(done.sem, 1)

            def body(c, last):
                if not last:
                    root(c + 1, varied, rooted)
                if not final:
                    root(c, varied_again, rooted_again)
                fetch.cut(pool, c)

            root(0, varied, rooted)
            with pool.Fori(0, NCH - 1) as c:
                body(c, False)
            body(NCH - 1, True)

        @block.scalar
        def _(act):
            def flip_out(c):
                act.wait_ge(flipped.sem, flipped.at(c, 1))
                for t in range(CT):
                    last = act.activation(turned[:, t, :], ps_t[t][:, :], ACT.Identity,
                                          bias=kit.column(offset_, t), scale=kit.column(gain_, t))
                last.then_inc(shaped.sem, 1)

            def body(c, last):
                for f in range(FT):
                    act.wait_ge(up.sem, up.at(c, f + 1))
                    act.wait_ge(hid_cut.sem, hid_cut.at(c, 2 * (f - 1)))
                    act.activation(act_out[f % 2][:, :], ps_h[f % 2][:, :], ACT.Gelu,
                                   bias=kit.column(up_bias, f)).then_inc(bent.sem, 1)
                if not last:
                    flip_out(c + 1)

            flip_out(0)
            with act.Fori(0, NCH - 1) as c:
                body(c, False)
            body(NCH - 1, True)

        @block.vector
        def _(dve):
            def vary(c, seen, src):
                for i in range(CK):
                    last = dve.bn_stats(stats[:, i, :], src[:, c * CK + i, :])
                last.then_inc(seen.sem, 1)
                dve.wait_ge(seen.sem, seen.at(c, 1))
                kit.apart(dve)
                for i in range(CK):
                    last = dve.bn_aggr(mean_var[:, i, :], stats[:, i, :])
                last.then_inc(seen.sem, 1)
                dve.wait_ge(seen.sem, seen.at(c, 2))
                dve.tensor_scalar(spread[:, :], mean_var[:, :, 1], EPS, None, ALU.add).then_inc(seen.sem, 1)

            def norm(c):
                dve.wait_ge(rooted.sem, rooted.at(c, 1))
                dve.wait_ge(flipped.sem, flipped.at(c, 0))
                for i in range(CK):
                    last = dve.tensor_scalar(n_in[:, i, :], kit.xo[:, c * CK + i, :], mean_var[:, i, 0:1],
                                             rstd[:, i:i + 1], ALU.subtract, ALU.mult)
                last.then_inc(normed.sem, 1)

            def flip_out(c):
                dve.wait_ge(shaped.sem, shaped.at(c, 1))
                dve.tensor_copy(x_in[0][:, :, :], turned[:, :, :]).then_inc(cut.sem, 1)
                dve.wait_ge(cut.sem, cut.at(c, 1))
                dve.tensor_tensor(x_in[1][:, :, :], turned[:, :, :], x_in[0][:, :, :].bitcast(F32), ALU.subtract
                                  ).then_inc(cut.sem, 1)

            def split(c, f):
                dve.wait_ge(bent.sem, bent.at(c, f + 1))
                dve.wait_ge(down.sem, down.at(c, f - 3))
                hi, lo = hid[f % 4]
                dve.tensor_copy(hi[:, :], act_out[f % 2][:, :]).then_inc(hid_cut.sem, 1)
                dve.wait_ge(hid_cut.sem, hid_cut.at(c, 2 * f + 1))
                dve.tensor_tensor(lo[:, :], act_out[f % 2][:, :], hi[:, :].bitcast(F32), ALU.subtract
                                  ).then_inc(hid_cut.sem, 1)

            def residual(c):
                ts = bass.ds(c * CK, CK)
                dve.tensor_tensor(kit.xo[:, ts, :], kit.xo[:, ts, :], kit.x1[:, ts, :], ALU.add).then_inc(summed.sem, 1)
                dve.wait_ge(summed.sem, summed.at(c, 1))
                if final:
                    dve.tensor_tensor(kit.x[:, ts, :], kit.x[:, ts, :], kit.xo[:, ts, :], ALU.add).then_inc(summed.sem, 1)
                    dve.wait_ge(summed.sem, summed.at(c, 2))
                to = kit.x if final else kit.xo
                for i in range(CK):
                    last = dve.tensor_tensor(to[:, c * CK + i, :], to[:, c * CK + i, :], rows[down_bias][:, :], ALU.add)
                last.then_inc(summed.sem, 1)

            def store(c):
                dve.wait_ge(summed.sem, summed.at(c, summed.per))
                dve.wait_ge(down.sem, down.at(c, FT))
                frm, to = (kit.x, kit.x) if final else (kit.xo, kit.x1)
                for i in range(CK):
                    last = dve.tensor_tensor(to[:, c * CK + i, :], ps_y[i][:, 0:C], frm[:, c * CK + i, :], ALU.add)
                last.then_inc(stored.sem, 1)

            def renorm(c):
                dve.wait_ge(stored.sem, stored.at(c, 1))
                kit.apart(dve)
                vary(c, varied_again, kit.x1)
                dve.wait_ge(rooted_again.sem, rooted_again.at(c, 1))
                for i in range(CK):
                    t = kit.x1[:, c * CK + i, :]
                    last = dve.tensor_scalar(t, t, mean_var[:, i, 0:1], rstd[:, i:i + 1], ALU.subtract, ALU.mult)
                last.then_inc(regained.sem, 1)
                dve.wait_ge(regained.sem, regained.at(c, 1))
                for i in range(CK):
                    t = kit.x1[:, c * CK + i, :]
                    last = dve.tensor_tensor(t, t, rows["ln2_g"][:, :], ALU.mult)
                last.then_inc(regained.sem, 1)
                dve.wait_ge(regained.sem, regained.at(c, 2))
                for i in range(CK):
                    t = kit.x1[:, c * CK + i, :]
                    dve.tensor_tensor(t, t, rows["ln2_b"][:, :], ALU.add)

            def body(c, last):
                split(c, 2)
                residual(c)
                split(c, 3)
                split(c, 4)
                if not last:
                    vary(c + 1, varied, kit.xo)
                split(c, 5)
                split(c, 6)
                if not last:
                    norm(c + 1)
                split(c, 7)
                if not last:
                    flip_out(c + 1)
                store(c)
                if not last:
                    split(c + 1, 0)
                    split(c + 1, 1)
                if not final:
                    renorm(c)

            dve.wait_ge(rows_in.sem, rows_in.at(0, len(rows)))
            if final:
                dve.wait_ge(x_back.sem, x_back.at(0, 1))
            vary(0, varied, kit.xo)
            norm(0)
            flip_out(0)
            split(0, 0)
            split(0, 1)
            with dve.Fori(0, NCH - 1) as c:
                body(c, False)
            body(NCH - 1, True)

        @block.tensor
        def _(pe):
            def flip(c):
                pe.wait_ge(normed.sem, normed.at(c, 1))
                for t in range(CT):
                    for i in range(CK):
                        last = pe.transpose(ps_t[t][:, i * P:(i + 1) * P], n_in[:, i, t * P:(t + 1) * P], kit.ident[:, :])
                last.then_inc(flipped.sem, 1)

            def rise(c, f):
                if f == 0:
                    pe.wait_ge(cut.sem, cut.at(c, 2))
                pe.wait_ge(bent.sem, bent.at(c, f - 1))
                for t in range(CT):
                    last = product(pe, ps_h[f % 2][:, :], kit.weights(w_up + t * FF + f * P, P),
                                   [x[:, t, :] for x in x_in], t == 0, t == CT - 1)
                last.then_inc(up.sem, 1)

            def fall(c, f):
                if f == 0:
                    pe.wait_ge(stored.sem, stored.at(c, 0))
                pe.wait_ge(hid_cut.sem, hid_cut.at(c, 2 * f + 2))
                for i in range(CK):
                    last = product(pe, ps_y[i][:, 0:C], [h[:, i * P:(i + 1) * P] for h in hid[f % 4]],
                                   kit.weights(w_down + f * C, C), f == 0, f == FT - 1)
                last.then_inc(down.sem, 1)

            def body(c, last):
                rise(c, 0)
                for f in range(1, FT):
                    rise(c, f)
                    if f < FT - 1:
                        fall(c, f - 1)
                if not last:
                    flip(c + 1)
                fall(c, FT - 2)
                fall(c, FT - 1)

            flip(0)
            with pe.Fori(0, NCH - 1) as c:
                body(c, False)
            body(NCH - 1, True)

    fetch.end()
    rows_in.end(1)
    if final:
        x_back.end(1)
    if not final:
        for s_ in (varied_again, rooted_again, regained):
            s_.end(NCH)
    for s_ in (varied, rooted, normed, flipped, shaped, cut, up, bent, hid_cut, down, summed, stored):
        s_.end(NCH)


def route(kit, dve, made, n, k, scores, count, tmp, seen):
    shape = [P, seen, E, E]
    rival = scores.unsqueeze(2).broadcast_to(shape)
    own = scores.unsqueeze(3).broadcast_to(shape)
    dve.tensor_tensor(tmp[0], rival, own, ALU.is_gt).then_inc(made.sem, 1)
    dve.tensor_tensor(tmp[1], rival, own, ALU.is_equal).then_inc(made.sem, 1)
    dve.wait_ge(made.sem, made.at(n, k + 2))
    for i in range(seen):
        last = dve.tensor_tensor(tmp[1][:, i], tmp[1][:, i], kit.lower[:, :, :], ALU.mult)
    last.then_inc(made.sem, 1)
    dve.wait_ge(made.sem, made.at(n, k + 3))
    dve.tensor_tensor(tmp[0], tmp[0], tmp[1], ALU.add).then_inc(made.sem, 1)
    dve.wait_ge(made.sem, made.at(n, k + 4))
    dve.tensor_reduce(count, tmp[0], AX.X, ALU.add).then_inc(made.sem, 1)
    dve.wait_ge(made.sem, made.at(n, k + 5))
    dve.tensor_scalar(count, count, TOP - 0.5, None, ALU.is_lt).then_inc(made.sem, 1)
    dve.wait_ge(made.sem, made.at(n, k + 6))
    return k + 6


def router(kit, own, pre, x_all, gates):
    nc, dram, tag = kit.nc, kit.dram, "router"
    w_up, w_down = own, own + CT * FF

    with ExitStack() as ctx:
        work = Space(nc, tag, kit.rest)
        n_in = work.take("n_in", [P, CK, C])
        act_out = [work.take(f"act_out{s}", [P, CHUNK]) for s in range(2)]
        hid = [[work.take(f"hid_{p}{s}", [P, CHUNK], F32R) for p in ("hi", "lo")] for s in range(4)]
        stats = work.take("stats", [P, CK, 6])
        mean_var = work.take("mean_var", [P, CK, 2])
        spread = work.take("spread", [P, CK])
        rstd = work.take("rstd", [P, CK])
        bias = work.take("bias", [P, E])
        scores = work.take("scores", [P, CK, E])
        chosen = work.take("chosen", [P, CK, E])
        highest = work.take("highest", [P, CK])
        tmp = [work.take(f"tmp{k}", [P, CK, E, E]) for k in range(2)]
        ps_y = [ctx.enter_context(nc.psum_tensor(f"{tag}_ps_y{i}", [P, 512], F32)) for i in range(CK)]
        ps_h = [ctx.enter_context(nc.psum_tensor(f"{tag}_ps_h{s}", [P, CHUNK], F32)) for s in range(2)]
        ps_t = ctx.enter_context(nc.psum_tensor(f"{tag}_ps_t", [P, CT, CHUNK], F32))

        rows_in = kit.counter("rows_in")
        varied = kit.counter("varied")
        rooted = kit.counter("rooted")
        normed = kit.counter("normed")
        flipped = kit.counter("flipped")
        shaped = kit.counter("shaped")
        cut = kit.counter("cut")
        up = kit.counter("up")
        bent = kit.counter("bent")
        hid_cut = kit.counter("hid_cut")
        down = kit.counter("down")
        gated = kit.counter("gated")
        grown = kit.counter("grown")
        rows_in.begin(1)
        ctx_in = kit.counter("ctx_in")
        ctx_in.begin(1)
        varied.begin(3)
        rooted.begin(1)
        normed.begin(1)
        flipped.begin(1)
        shaped.begin(1)
        cut.begin(1)
        up.begin(FT)
        bent.begin(FT)
        hid_cut.begin(2 * FT)
        down.begin(FT)
        gated.begin(13)
        grown.begin(1)
        fetch = Prefetch(kit, *pre, NCH)
        block = ctx.enter_context(nc.Block())

        @block.sync
        def _(sp):
            sp.dma_start(bias[:, :], dram["rb2"].broadcast_to([P, E])).then_inc(rows_in.sem, 16)
            sp.dma_start(kit.ctx_t[:, :], dram["ctx_t"]).then_inc(ctx_in.sem, 16)
            with sp.Fori(0, NCH) as c:
                fetch.load(sp, c)
            sp.wait_ge(ctx_in.sem, ctx_in.at(0, 1))

        @block.gpsimd
        def _(pool):
            def root(c):
                pool.wait_ge(varied.sem, varied.at(c, 3))
                pool.tensor_tensor(rstd[:, :], spread[:, :], kit.power[:, 0:CK], ALU.pow).then_inc(rooted.sem, 1)

            root(0)
            with pool.Fori(0, NCH - 1) as c:
                root(c + 1)
                fetch.cut(pool, c)
            fetch.cut(pool, NCH - 1)

        @block.scalar
        def _(act):
            def flip_out(c):
                act.wait_ge(flipped.sem, flipped.at(c, 1))
                act.activation(x_all[0][:, :, bass.ds(c * CHUNK, CHUNK)], ps_t[:, :, :], ACT.Identity
                               ).then_inc(shaped.sem, 1)

            def body(c, last):
                for f in range(FT):
                    act.wait_ge(up.sem, up.at(c, f + 1))
                    act.wait_ge(hid_cut.sem, hid_cut.at(c, 2 * (f - 1)))
                    act.activation(act_out[f % 2][:, :], ps_h[f % 2][:, :], ACT.Relu,
                                   bias=kit.column("rb1", f)).then_inc(bent.sem, 1)
                if not last:
                    flip_out(c + 1)
                act.wait_ge(gated.sem, gated.at(c, 9))
                act.activation(scores[:, :, :], scores[:, :, :], ACT.Exp).then_inc(grown.sem, 1)

            flip_out(0)
            with act.Fori(0, NCH - 1) as c:
                body(c, False)
            body(NCH - 1, True)

        @block.vector
        def _(dve):
            def vary(c):
                for i in range(CK):
                    last = dve.bn_stats(stats[:, i, :], kit.x[:, c * CK + i, :])
                last.then_inc(varied.sem, 1)
                dve.wait_ge(varied.sem, varied.at(c, 1))
                kit.apart(dve)
                for i in range(CK):
                    last = dve.bn_aggr(mean_var[:, i, :], stats[:, i, :])
                last.then_inc(varied.sem, 1)
                dve.wait_ge(varied.sem, varied.at(c, 2))
                dve.tensor_scalar(spread[:, :], mean_var[:, :, 1], EPS, None, ALU.add).then_inc(varied.sem, 1)

            def norm(c):
                dve.wait_ge(rooted.sem, rooted.at(c, 1))
                dve.wait_ge(flipped.sem, flipped.at(c, 0))
                for i in range(CK):
                    last = dve.tensor_scalar(n_in[:, i, :], kit.x[:, c * CK + i, :], mean_var[:, i, 0:1],
                                             rstd[:, i:i + 1], ALU.subtract, ALU.mult)
                last.then_inc(normed.sem, 1)

            def flip_out(c):
                dve.wait_ge(shaped.sem, shaped.at(c, 1))
                at = bass.ds(c * CHUNK, CHUNK)
                dve.tensor_tensor(x_all[1][:, :, at], ps_t[:, :, :], x_all[0][:, :, at].bitcast(F32), ALU.subtract
                                  ).then_inc(cut.sem, 1)

            def split(c, f):
                dve.wait_ge(bent.sem, bent.at(c, f + 1))
                dve.wait_ge(down.sem, down.at(c, f - 3))
                hi, lo = hid[f % 4]
                dve.tensor_copy(hi[:, :], act_out[f % 2][:, :]).then_inc(hid_cut.sem, 1)
                dve.wait_ge(hid_cut.sem, hid_cut.at(c, 2 * f + 1))
                dve.tensor_tensor(lo[:, :], act_out[f % 2][:, :], hi[:, :].bitcast(F32), ALU.subtract
                                  ).then_inc(hid_cut.sem, 1)

            def gate(c):
                dve.wait_ge(down.sem, down.at(c, FT))
                for i in range(CK):
                    last = dve.tensor_tensor(scores[:, i, :], ps_y[i][:, 0:E], bias[:, :], ALU.add)
                last.then_inc(gated.sem, 1)
                dve.wait_ge(gated.sem, gated.at(c, 1))
                k = route(kit, dve, gated, c, 1, scores[:, :, :], chosen[:, :, :], [t[:, :, :, :] for t in tmp], CK)
                assert k == 7
                wide = [P, CK, E]
                dve.tensor_reduce(highest[:, :], scores[:, :, :], AX.X, ALU.max).then_inc(gated.sem, 1)
                dve.wait_ge(gated.sem, gated.at(c, 8))
                dve.tensor_tensor(scores[:, :, :], scores[:, :, :], highest[:, :].unsqueeze(2).broadcast_to(wide),
                                  ALU.subtract).then_inc(gated.sem, 1)
                dve.wait_ge(grown.sem, grown.at(c, 1))
                dve.tensor_tensor(chosen[:, :, :], chosen[:, :, :], scores[:, :, :], ALU.mult).then_inc(gated.sem, 1)
                dve.wait_ge(gated.sem, gated.at(c, 10))
                dve.tensor_reduce(highest[:, :], chosen[:, :, :], AX.X, ALU.add).then_inc(gated.sem, 1)
                dve.wait_ge(gated.sem, gated.at(c, 11))
                dve.reciprocal(highest[:, :], highest[:, :]).then_inc(gated.sem, 1)
                dve.wait_ge(gated.sem, gated.at(c, 12))
                dve.tensor_tensor(gates[:, bass.ds(c * CK, CK), :], chosen[:, :, :],
                                  highest[:, :].unsqueeze(2).broadcast_to(wide), ALU.mult).then_inc(gated.sem, 1)

            def body(c, last):
                split(c, 2)
                split(c, 3)
                split(c, 4)
                if not last:
                    vary(c + 1)
                split(c, 5)
                split(c, 6)
                if not last:
                    norm(c + 1)
                split(c, 7)
                if not last:
                    flip_out(c + 1)
                gate(c)
                if not last:
                    split(c + 1, 0)
                    split(c + 1, 1)

            dve.wait_ge(rows_in.sem, rows_in.at(0, 1))
            vary(0)
            norm(0)
            flip_out(0)
            split(0, 0)
            split(0, 1)
            with dve.Fori(0, NCH - 1) as c:
                body(c, False)
            body(NCH - 1, True)

        @block.tensor
        def _(pe):
            def flip(c):
                pe.wait_ge(normed.sem, normed.at(c, 1))
                for t in range(CT):
                    for i in range(CK):
                        last = pe.transpose(ps_t[:, t, i * P:(i + 1) * P], n_in[:, i, t * P:(t + 1) * P], kit.ident[:, :])
                last.then_inc(flipped.sem, 1)

            def rise(c, f):
                if f == 0:
                    pe.wait_ge(cut.sem, cut.at(c, 1))
                pe.wait_ge(bent.sem, bent.at(c, f - 1))
                at = bass.ds(c * CHUNK, CHUNK)
                for t in range(CT):
                    last = product(pe, ps_h[f % 2][:, :], kit.weights(w_up + t * FF + f * P, P),
                                   [x[:, t, at] for x in x_all], t == 0, t == CT - 1)
                last.then_inc(up.sem, 1)

            def fall(c, f):
                if f == 0:
                    pe.wait_ge(gated.sem, gated.at(c, 0))
                pe.wait_ge(hid_cut.sem, hid_cut.at(c, 2 * f + 2))
                for i in range(CK):
                    last = product(pe, ps_y[i][:, 0:E], [h[:, i * P:(i + 1) * P] for h in hid[f % 4]],
                                   kit.weights(w_down + f * E, E), f == 0, f == FT - 1)
                last.then_inc(down.sem, 1)

            def body(c, last):
                rise(c, 0)
                for f in range(1, FT):
                    rise(c, f)
                    if f < FT - 1:
                        fall(c, f - 1)
                if not last:
                    flip(c + 1)
                fall(c, FT - 2)
                fall(c, FT - 1)

            flip(0)
            with pe.Fori(0, NCH - 1) as c:
                body(c, False)
            body(NCH - 1, True)

    fetch.end()
    rows_in.end(1)
    ctx_in.end(1)
    for s_ in (varied, rooted, normed, flipped, shaped, cut, up, bent, hid_cut, down, gated, grown):
        s_.end(NCH)


def experts(kit, slots, src, x_all, gates):
    nc, dram, tag = kit.nc, kit.dram, "experts"

    with ExitStack() as ctx:
        work = Space(nc, tag, [*kit.slot_ranges[1], *kit.rest])
        act_out = [work.take(f"act_out{s}", [P, CHUNK]) for s in range(2)]
        hid = [[work.take(f"hid_{p}{s}", [P, CHUNK], F32R) for p in ("hi", "lo")] for s in range(4)]
        bias = work.take("bias", [P, E * C], F32R)
        bias_raw = work.take("bias_raw", [1, E * C])
        bias_lo = work.take("bias_lo", [1, E * C], F32R)
        ps_y = [ctx.enter_context(nc.psum_tensor(f"{tag}_ps_y{i}", [P, 512], F32)) for i in range(CK)]
        ps_h = [ctx.enter_context(nc.psum_tensor(f"{tag}_ps_h{s}", [P, CHUNK], F32)) for s in range(4)]

        rows_in = kit.counter("rows_in")
        row_moved = kit.counter("x_in")
        up = kit.counter("up")
        bent = kit.counter("bent")
        hid_cut = kit.counter("hid_cut")
        down = kit.counter("down")
        stored = kit.counter("stored")
        made = kit.counter("set_up_v")
        zeroed = kit.counter("set_up")
        n_steps = NCH * FT
        rows_in.begin(1)
        row_moved.begin(1)
        up.begin(n_steps)
        bent.begin(n_steps)
        hid_cut.begin(2 * n_steps)
        down.begin(n_steps)
        stored.begin(NCH)
        made.begin(2)
        zeroed.begin(1)
        w_split, w_landed = kit.w_split, kit.w_landed
        w_split.begin(2 * SLOT // PIECE)
        for s in w_landed:
            s.begin(SLOT // PIECE // 2)
        block = ctx.enter_context(nc.Block())

        @block.sync
        def _(sp):
            sp.dma_start(bias_raw[:, :], dram["b2"]).then_inc(rows_in.sem, 16)

            def load(e):
                for k in range(SLOT // PIECE):
                    sp.wait_ge(w_split.sem, w_split.at(e, 2 * (k - 1)))
                    sp.dma_start(kit.raw[k % 2][:, :], src[e + 1, :, k * PIECE:(k + 1) * PIECE]
                                 ).then_inc(w_landed[k % 2].sem, 16)

            load(0)
            sp.wait_ge(made.sem, made.at(0, 2))
            sp.dma_start(bias[1:2, :].bitcast(F32), bias_lo[:, :].bitcast(F32)).then_inc(row_moved.sem, 16)
            load(1)
            with sp.Fori(1, E // 2) as pair:
                load(2 * pair)
                load(2 * pair + 1)

        @block.gpsimd
        def _(pool):
            pool.memset(bias[:, :].bitcast(F32), 0.0).then_inc(zeroed.sem, 1)

            def cut(e, slot):
                for k in range(SLOT // PIECE):
                    raw = kit.raw[k % 2][:, :]
                    at = bass.ds(slot + k * PIECE, PIECE)
                    pool.wait_ge(w_landed[k % 2].sem, w_landed[k % 2].at(e, k // 2 + 1))
                    if k == 0:
                        pool.wait_ge(stored.sem, stored.at(e, 0))
                    kit.apart(pool)
                    pool.tensor_copy(kit.w_hi[:, at], raw).then_inc(w_split.sem, 1)
                    pool.wait_ge(w_split.sem, w_split.at(e, 2 * k + 1))
                    pool.tensor_tensor(kit.w_lo[:, at], raw, kit.w_hi[:, at].bitcast(F32), ALU.subtract
                                       ).then_inc(w_split.sem, 1)

            with pool.Fori(0, E // 2) as pair:
                cut(2 * pair, slots[1])
                cut(2 * pair + 1, slots[0])

        @block.scalar
        def _(act):
            with act.Fori(0, E // 2) as pair:
                for odd in range(2):
                    e = 2 * pair + odd
                    for n in range(n_steps):
                        act.wait_ge(up.sem, up.at(e, n + 1))
                        act.wait_ge(hid_cut.sem, hid_cut.at(e, 2 * (n - 1)))
                        kit.apart(act)
                        at = kit.dram["col_at"]["b1"]
                        act.activation(act_out[n % 2][:, :], ps_h[n % 4][:, :], ACT.Relu,
                                       bias=kit.cols[:, bass.ds(e * FT + (at + n % FT), 1)]).then_inc(bent.sem, 1)

        @block.vector
        def _(dve):
            dve.wait_ge(rows_in.sem, rows_in.at(0, 1))
            dve.wait_ge(zeroed.sem, zeroed.at(0, 1))
            dve.tensor_copy(bias[0:1, :], bias_raw[:, :]).then_inc(made.sem, 1)
            dve.wait_ge(made.sem, made.at(0, 1))
            dve.tensor_tensor(bias_lo[:, :], bias_raw[:, :], bias[0:1, :].bitcast(F32), ALU.subtract
                              ).then_inc(made.sem, 1)

            def split(e, n):
                dve.wait_ge(bent.sem, bent.at(e, n + 1))
                dve.wait_ge(down.sem, down.at(e, n - 3))
                hi, lo = hid[n % 4]
                dve.tensor_copy(hi[:, :], act_out[n % 2][:, :]).then_inc(hid_cut.sem, 1)
                dve.wait_ge(hid_cut.sem, hid_cut.at(e, 2 * n + 1))
                dve.tensor_tensor(lo[:, :], act_out[n % 2][:, :], hi[:, :].bitcast(F32), ALU.subtract
                                  ).then_inc(hid_cut.sem, 1)

            def store(e, c):
                dve.wait_ge(down.sem, down.at(e, (c + 1) * FT))
                for i in range(CK):
                    t = c * CK + i
                    last = dve.scalar_tensor_tensor(kit.x[:, t, :], ps_y[i][:, 0:C], gates[:, t, bass.ds(e, 1)],
                                                    kit.x[:, t, :], ALU.mult, ALU.add)
                last.then_inc(stored.sem, 1)

            with dve.Fori(0, E // 2) as pair:
                for odd in range(2):
                    e = 2 * pair + odd
                    for n in range(n_steps):
                        split(e, n)
                        if n % FT == 0 and n:
                            store(e, n // FT - 1)
                    store(e, NCH - 1)

        @block.tensor
        def _(pe):
            def rise(e, slot, n):
                c, f = n // FT, n % FT
                pe.wait_ge(bent.sem, bent.at(e, n - 3))
                for t in range(CT):
                    last = product(pe, ps_h[n % 4][:, :], kit.weights(slot + t * FF + f * P, P),
                                   [x[:, t, c * CHUNK:(c + 1) * CHUNK] for x in x_all], t == 0, t == CT - 1)
                last.then_inc(up.sem, 1)

            def fall(e, slot, n):
                c, f = n // FT, n % FT
                if f == 0:
                    pe.wait_ge(stored.sem, stored.at(e, c))
                pe.wait_ge(hid_cut.sem, hid_cut.at(e, 2 * n + 2))
                for i in range(CK):
                    if f == 0:
                        pe.matmul(ps_y[i][:, 0:C], kit.pick[:, :], bias[:, bass.ds(e * C, C)], start=True, stop=False)
                    last = product(pe, ps_y[i][:, 0:C], [h[:, i * P:(i + 1) * P] for h in hid[n % 4]],
                                   kit.weights(slot + CT * FF + f * C, C), False, f == FT - 1)
                last.then_inc(down.sem, 1)

            pe.wait_ge(row_moved.sem, row_moved.at(0, 1))
            with pe.Fori(0, E // 2) as pair:
                for odd in range(2):
                    e, slot = 2 * pair + odd, slots[odd]
                    pe.wait_ge(w_split.sem, w_split.at(e, 0))
                    rise(e, slot, 0)
                    for n in range(1, n_steps):
                        rise(e, slot, n)
                        fall(e, slot, n - 1)
                    fall(e, slot, n_steps - 1)

    w_split.end(E)
    for s_ in w_landed:
        s_.end(E)
    for s_ in (rows_in, row_moved, made, zeroed):
        s_.end(1)
    for s_ in (up, bent, hid_cut, down, stored):
        s_.end(E)


def tree(kit, own, pre):
    nc, dram, tag = kit.nc, kit.dram, "tree"
    pairs = NT // 2
    w_in, w_out = own, own + SLOT
    bank = NODES // 4
    wide = TREE_T * P

    with ExitStack() as ctx:
        work = Space(nc, tag, kit.late)
        n_in = work.take("n_in", [P, 2, C])
        x_in = [work.take(f"x_{p}", [P, CT, 2 * P], F32R) for p in ("hi", "lo")]
        bias = work.take("bias", [P, NODES], F32R)
        value = [work.take(f"value{s}", [P, wide]) for s in range(2)]
        right = [work.take(f"right{s}", [P, NODES]) for s in range(2)]
        active = work.take("active", [P, TREES, TREE])
        leaf = [work.take(f"leaf_{p}", [P, TREE_T, P], F32R) for p in ("hi", "lo")]
        stats = work.take("stats", [P, 2, 6])
        mean_var = work.take("mean_var", [P, 2, 2])
        spread = work.take("spread", [P, 2])
        rstd = work.take("rstd", [P, 2])
        ps_logit = ctx.enter_context(nc.psum_tensor(f"{tag}_ps_logit", [P, 4, 512], F32))
        ps_turn = ctx.enter_context(nc.psum_tensor(f"{tag}_ps_turn", [P, TREE_T // 2, P], F32))
        ps_y = ctx.enter_context(nc.psum_tensor(f"{tag}_ps_y", [P, 512], F32))
        ps_t = ctx.enter_context(nc.psum_tensor(f"{tag}_ps_t", [P, CT, 2 * P], F32))

        rows_in = kit.counter("rows_in")
        row_moved = kit.counter("x_in")
        planted = kit.counter("planted")
        zeroed = kit.counter("set_up")
        varied = kit.counter("varied")
        rooted = kit.counter("rooted")
        normed = kit.counter("normed")
        flipped = kit.counter("flipped")
        shaped = kit.counter("shaped")
        cut = kit.counter("cut")
        up = kit.counter("up")
        judged = kit.counter("judged")
        valued = kit.counter("valued")
        walked = kit.counter("walked")
        veiled = kit.counter("veiled")
        turned_out = kit.counter("turned_out")
        leaf_high = kit.counter("leaf_high")
        leaf_low = kit.counter("leaf_low")
        gathered = kit.counter("gathered")
        stored = kit.counter("stored")
        rows_in.begin(1)
        row_moved.begin(1)
        planted.begin(5)
        zeroed.begin(1)
        varied.begin(3)
        for s_ in (rooted, normed, flipped, shaped, cut):
            s_.begin(1)
        for s_ in (up, judged, valued, veiled, gathered, stored):
            s_.begin(2)
        walked.begin(2 * 2 * DEPTH)
        for s_ in (turned_out, leaf_high, leaf_low):
            s_.begin(4)
        fetch = Prefetch(kit, *pre, pairs)
        bias_raw, bias_lo = right[0], leaf[0][0:1, :, :].rearrange("p t n -> p (t n)")
        block = ctx.enter_context(nc.Block())

        @block.sync
        def _(sp):
            sp.dma_start(bias_raw[0:1, :], dram["tree_bias"]).then_inc(rows_in.sem, 16)
            sp.wait_ge(planted.sem, planted.at(0, 2))
            sp.dma_start(bias[1:2, :].bitcast(F32), bias_lo[:, 0:NODES].bitcast(F32)).then_inc(row_moved.sem, 16)
            with sp.Fori(0, pairs) as p:
                fetch.load(sp, p)

        @block.gpsimd
        def _(pool):
            pool.memset(bias[:, :].bitcast(F32), 0.0).then_inc(zeroed.sem, 1)

            def root(p):
                pool.wait_ge(varied.sem, varied.at(p, 3))
                pool.tensor_tensor(rstd[:, :], spread[:, :], kit.power[:, 0:2], ALU.pow).then_inc(rooted.sem, 1)

            root(0)
            with pool.Fori(0, pairs - 1) as p:
                root(p + 1)
                fetch.cut(pool, p)
            fetch.cut(pool, pairs - 1)

        @block.scalar
        def _(act):
            def flip_out(p):
                act.wait_ge(flipped.sem, flipped.at(p, 1))
                act.activation(x_in[0][:, :, :], ps_t[:, :, :], ACT.Identity).then_inc(shaped.sem, 1)

            def evaluate(p, i):
                act.wait_ge(up.sem, up.at(p, i + 1))
                act.wait_ge(judged.sem, judged.at(p, i + 1))
                act.wait_ge(turned_out.sem, turned_out.at(p, 2 * i - 2))
                act.activation(value[i][:, 0:NODES].rearrange("p (k n) -> p k n", k=4), ps_logit[:, :, 0:bank], ACT.Silu
                               ).then_inc(valued.sem, 1)

            def high(p, i):
                for r in range(2):
                    act.wait_ge(turned_out.sem, turned_out.at(p, 2 * i + r + 1))
                    act.activation(leaf[0][:, r * TREE_T // 2:(r + 1) * TREE_T // 2, :], ps_turn[:, :, :], ACT.Identity
                                   ).then_inc(leaf_high.sem, 1)

            def body(p, last):
                if not last:
                    flip_out(p + 1)
                for i in range(2):
                    high(p, i)
                    if not last:
                        evaluate(p + 1, i)

            act.wait_ge(planted.sem, planted.at(0, 5))
            flip_out(0)
            evaluate(0, 0)
            evaluate(0, 1)
            with act.Fori(0, pairs - 1) as p:
                body(p, False)
            body(pairs - 1, True)

        @block.vector
        def _(dve):
            dve.wait_ge(rows_in.sem, rows_in.at(0, 1))
            dve.wait_ge(zeroed.sem, zeroed.at(0, 1))
            dve.tensor_copy(bias[0:1, :], bias_raw[0:1, :]).then_inc(planted.sem, 1)
            dve.wait_ge(planted.sem, planted.at(0, 1))
            dve.tensor_tensor(bias_lo[:, 0:NODES], bias_raw[0:1, :], bias[0:1, :].bitcast(F32), ALU.subtract
                              ).then_inc(planted.sem, 1)
            for s in range(2):
                dve.memset(value[s][:, NODES:wide], 0.0).then_inc(planted.sem, 1)
            dve.memset(active[:, :, 0:1], 1.0).then_inc(planted.sem, 1)
            dve.wait_ge(row_moved.sem, row_moved.at(0, 1))
            dve.wait_ge(planted.sem, planted.at(0, 5))

            def vary(p):
                for i in range(2):
                    last = dve.bn_stats(stats[:, i, :], kit.x[:, p * 2 + i, :])
                last.then_inc(varied.sem, 1)
                dve.wait_ge(varied.sem, varied.at(p, 1))
                kit.apart(dve)
                for i in range(2):
                    last = dve.bn_aggr(mean_var[:, i, :], stats[:, i, :])
                last.then_inc(varied.sem, 1)
                dve.wait_ge(varied.sem, varied.at(p, 2))
                dve.tensor_scalar(spread[:, :], mean_var[:, :, 1], EPS, None, ALU.add).then_inc(varied.sem, 1)

            def norm(p):
                dve.wait_ge(rooted.sem, rooted.at(p, 1))
                dve.wait_ge(flipped.sem, flipped.at(p, 0))
                for i in range(2):
                    last = dve.tensor_scalar(n_in[:, i, :], kit.x[:, p * 2 + i, :], mean_var[:, i, 0:1],
                                             rstd[:, i:i + 1], ALU.subtract, ALU.mult)
                last.then_inc(normed.sem, 1)

            def flip_out(p):
                dve.wait_ge(shaped.sem, shaped.at(p, 1))
                dve.tensor_tensor(x_in[1][:, :, :], ps_t[:, :, :], x_in[0][:, :, :].bitcast(F32), ALU.subtract
                                  ).then_inc(cut.sem, 1)

            def judge(p, i):
                dve.wait_ge(up.sem, up.at(p, i + 1))
                dve.tensor_scalar(right[i][:, :].rearrange("p (k n) -> p k n", k=4), ps_logit[:, :, 0:bank], 0.0, None,
                                  ALU.is_gt).then_inc(judged.sem, 1)

            def walk(p, i):
                goes = right[i][:, :].rearrange("p (t n) -> p t n", n=TREE)
                dve.wait_ge(judged.sem, judged.at(p, i + 1))
                for d in range(DEPTH):
                    at, n = 2 ** d - 1, 2 ** d
                    k = 2 * DEPTH * i + 2 * d
                    young = active[:, :, 2 * at + 1:2 * at + 1 + 2 * n].rearrange("p t (n two) -> p t n two", two=2)
                    dve.tensor_tensor(young[:, :, :, 1], active[:, :, at:at + n], goes[:, :, at:at + n], ALU.mult
                                      ).then_inc(walked.sem, 1)
                    dve.wait_ge(walked.sem, walked.at(p, k + 1))
                    dve.tensor_tensor(young[:, :, :, 0], active[:, :, at:at + n], young[:, :, :, 1], ALU.subtract
                                      ).then_inc(walked.sem, 1)
                    dve.wait_ge(walked.sem, walked.at(p, k + 2))
                dve.wait_ge(valued.sem, valued.at(p, i + 1))
                flat = active[:, :, :].rearrange("p t n -> p (t n)")
                dve.tensor_tensor(value[i][:, 0:NODES], value[i][:, 0:NODES], flat, ALU.mult).then_inc(veiled.sem, 1)

            def low(p, i):
                for r in range(2):
                    half = slice(r * TREE_T // 2, (r + 1) * TREE_T // 2)
                    dve.wait_ge(leaf_high.sem, leaf_high.at(p, 2 * i + r + 1))
                    dve.tensor_tensor(leaf[1][:, half, :], ps_turn[:, :, :], leaf[0][:, half, :].bitcast(F32),
                                      ALU.subtract).then_inc(leaf_low.sem, 1)

            def store(p, i):
                dve.wait_ge(gathered.sem, gathered.at(p, i + 1))
                t = kit.x[:, p * 2 + i, :]
                dve.tensor_tensor(t, ps_y[:, 0:C], t, ALU.add).then_inc(stored.sem, 1)

            def body(p, first, last):
                if not last:
                    vary(p + 1)
                    norm(p + 1)
                walk(p, 0)
                if not first:
                    store(p - 1, 1)
                if not last:
                    flip_out(p + 1)
                low(p, 0)
                if not last:
                    judge(p + 1, 0)
                walk(p, 1)
                store(p, 0)
                low(p, 1)
                if not last:
                    judge(p + 1, 1)

            vary(0)
            norm(0)
            flip_out(0)
            judge(0, 0)
            judge(0, 1)
            body(0, True, False)
            with dve.Fori(1, pairs - 1) as p:
                body(p, False, False)
            body(pairs - 1, False, True)
            store(pairs - 1, 1)

        @block.tensor
        def _(pe):
            def flip(p):
                pe.wait_ge(normed.sem, normed.at(p, 1))
                for t in range(CT):
                    for i in range(2):
                        last = pe.transpose(ps_t[:, t, i * P:(i + 1) * P], n_in[:, i, t * P:(t + 1) * P], kit.ident[:, :])
                last.then_inc(flipped.sem, 1)

            def logits(p, i):
                if i == 0:
                    pe.wait_ge(cut.sem, cut.at(p, 1))
                pe.wait_ge(valued.sem, valued.at(p, i))
                for k in range(4):
                    out = ps_logit[:, k, 0:bank]
                    pe.matmul(out, kit.pick[:, :], bias[:, k * bank:(k + 1) * bank], start=True, stop=False)
                    for t in range(CT):
                        last = product(pe, out, [x[:, t, i * P:(i + 1) * P] for x in x_in],
                                       kit.weights(w_in + t * NODES + k * bank, bank), False, t == CT - 1)
                last.then_inc(up.sem, 1)

            def turn(p, i):
                pe.wait_ge(veiled.sem, veiled.at(p, i + 1))
                for r in range(2):
                    pe.wait_ge(leaf_low.sem, leaf_low.at(p, 2 * i + r))
                    for n in range(TREE_T // 2):
                        at = (r * TREE_T // 2 + n) * P
                        last = pe.transpose(ps_turn[:, n, :], value[i][:, at:at + P], kit.ident[:, :])
                    last.then_inc(turned_out.sem, 1)

            def gather(p, i):
                pe.wait_ge(leaf_low.sem, leaf_low.at(p, 2 * i + 2))
                pe.wait_ge(stored.sem, stored.at(p, i))
                for n in range(TREE_T):
                    last = product(pe, ps_y[:, 0:C], [x[:, n, :] for x in leaf], kit.weights(w_out + n * C, C),
                                   n == 0, n == TREE_T - 1)
                last.then_inc(gathered.sem, 1)

            def body(p, last):
                if not last:
                    flip(p + 1)
                for i in range(2):
                    turn(p, i)
                    if not last:
                        logits(p + 1, i)
                    gather(p, i)

            pe.wait_ge(row_moved.sem, row_moved.at(0, 1))
            flip(0)
            logits(0, 0)
            logits(0, 1)
            with pe.Fori(0, pairs - 1) as p:
                body(p, False)
            body(pairs - 1, True)

    fetch.end()
    for s_ in (rows_in, row_moved, planted, zeroed):
        s_.end(1)
    for s_ in (varied, rooted, normed, flipped, shaped, cut, up, judged, valued, veiled, gathered, stored, walked,
               turned_out, leaf_high, leaf_low):
        s_.end(pairs)


def swiglu(kit, own, pre):
    nc, tag = kit.nc, "swiglu"
    units = E + CT
    w_gate, w_up, w_down = own, own + CT * E * P, own + 2 * CT * E * P
    s_gate = w_down + E * C
    s_up, s_down = s_gate + CT * C, s_gate + 2 * CT * C
    w_score = s_down + CT * C

    with ExitStack() as ctx:
        work = Space(nc, tag, kit.late)
        x_in = [work.take(f"x_in_{p}", [P, CT, CHUNK], F32R) for p in ("hi", "lo")]
        gates = work.take("gates", [P, NT, E])
        n_in = work.take("n_in", [P, CK, C])
        bent_out = [work.take(f"bent_out{s}", [P, CHUNK]) for s in range(2)]
        hid_one = [work.take(f"hid_one{s}", [P, CHUNK]) for s in range(2)]
        hid = [[work.take(f"hid_{p}{s}", [P, CHUNK], F32R) for p in ("hi", "lo")] for s in range(2)]
        stats = work.take("stats", [P, CK, 6])
        mean_var = work.take("mean_var", [P, CK, 2])
        spread = work.take("spread", [P, CK])
        rstd = work.take("rstd", [P, CK])
        scores = work.take("scores", [P, CK, E])
        chosen = work.take("chosen", [P, CK, E])
        total = work.take("total", [P, CK])
        tmp = [work.take(f"tmp{k}", [P, CK, E, E]) for k in range(2)]
        ps_g = [ctx.enter_context(nc.psum_tensor(f"{tag}_ps_g{s}", [P, CHUNK], F32)) for s in range(2)]
        ps_u = [ctx.enter_context(nc.psum_tensor(f"{tag}_ps_u{s}", [P, CHUNK], F32)) for s in range(2)]
        ps_y = ctx.enter_context(nc.psum_tensor(f"{tag}_ps_y", [P, CK, C], F32))
        ps_t = ctx.enter_context(nc.psum_tensor(f"{tag}_ps_t", [P, CT, CHUNK], F32))

        varied = kit.counter("varied")
        rooted = kit.counter("rooted")
        normed = kit.counter("normed")
        flipped = kit.counter("flipped")
        shaped = kit.counter("shaped")
        cut = kit.counter("cut")
        scored = kit.counter("scored")
        grown = kit.counter("grown")
        gated = kit.counter("gated")
        up = kit.counter("up")
        bent = kit.counter("bent")
        hid_cut = kit.counter("hid_cut")
        down = kit.counter("down")
        stored = kit.counter("stored")
        for s_ in (rooted, normed, flipped, shaped, cut, scored, grown):
            s_.begin(1)
        varied.begin(3)
        gated.begin(11)
        up.begin(2 * units)
        bent.begin(units)
        hid_cut.begin(3 * units)
        down.begin(E + 1)
        stored.begin(E + 1)
        fetch = Prefetch(kit, *pre, NCH)
        block = ctx.enter_context(nc.Block())

        @block.sync
        def _(sp):
            with sp.Fori(0, NCH) as c:
                fetch.load(sp, c)

        @block.gpsimd
        def _(pool):
            def root(c):
                pool.wait_ge(varied.sem, varied.at(c, 3))
                pool.tensor_tensor(rstd[:, :], spread[:, :], kit.power[:, 0:CK], ALU.pow).then_inc(rooted.sem, 1)

            root(0)
            with pool.Fori(0, NCH - 1) as c:
                root(c + 1)
                fetch.cut(pool, c)
            fetch.cut(pool, NCH - 1)

        @block.scalar
        def _(act):
            def flip_out(c):
                act.wait_ge(flipped.sem, flipped.at(c, 1))
                act.wait_ge(up.sem, up.at(c, 0))
                act.activation(x_in[0][:, :, :], ps_t[:, :, :], ACT.Identity).then_inc(shaped.sem, 1)

            def weigh(c):
                act.wait_ge(scored.sem, scored.at(c, 1))
                act.wait_ge(gated.sem, gated.at(c, 0))
                act.activation(scores[:, :, :].rearrange("p i e -> p (i e)"), ps_t[:, 0, 0:CK * E], ACT.Sigmoid
                               ).then_inc(grown.sem, 1)

            def bend(c, n):
                act.wait_ge(up.sem, up.at(c, 2 * n + 1))
                act.wait_ge(hid_cut.sem, hid_cut.at(c, 3 * n - 5))
                act.activation(bent_out[n % 2][:, :], ps_g[n % 2][:, :], ACT.Silu).then_inc(bent.sem, 1)

            def body(c, last):
                for n in range(1, units):
                    bend(c, n)
                if not last:
                    flip_out(c + 1)
                    weigh(c + 1)
                    bend(c + 1, 0)

            flip_out(0)
            weigh(0)
            bend(0, 0)
            with act.Fori(0, NCH - 1) as c:
                body(c, False)
            body(NCH - 1, True)

        @block.vector
        def _(dve):
            def vary(c):
                for i in range(CK):
                    last = dve.bn_stats(stats[:, i, :], kit.x[:, c * CK + i, :])
                last.then_inc(varied.sem, 1)
                dve.wait_ge(varied.sem, varied.at(c, 1))
                kit.apart(dve)
                for i in range(CK):
                    last = dve.bn_aggr(mean_var[:, i, :], stats[:, i, :])
                last.then_inc(varied.sem, 1)
                dve.wait_ge(varied.sem, varied.at(c, 2))
                dve.tensor_scalar(spread[:, :], mean_var[:, :, 1], EPS, None, ALU.add).then_inc(varied.sem, 1)

            def norm(c):
                dve.wait_ge(rooted.sem, rooted.at(c, 1))
                dve.wait_ge(flipped.sem, flipped.at(c, 0))
                for i in range(CK):
                    last = dve.tensor_scalar(n_in[:, i, :], kit.x[:, c * CK + i, :], mean_var[:, i, 0:1],
                                             rstd[:, i:i + 1], ALU.subtract, ALU.mult)
                last.then_inc(normed.sem, 1)

            def flip_out(c):
                dve.wait_ge(shaped.sem, shaped.at(c, 1))
                dve.tensor_tensor(x_in[1][:, :, :], ps_t[:, :, :], x_in[0][:, :, :].bitcast(F32), ALU.subtract
                                  ).then_inc(cut.sem, 1)

            def gate(c):
                dve.wait_ge(grown.sem, grown.at(c, 1))
                k = route(kit, dve, gated, c, 0, scores[:, :, :], chosen[:, :, :], [t[:, :, :, :] for t in tmp], CK)
                assert k == 6
                dve.tensor_tensor(chosen[:, :, :], chosen[:, :, :], scores[:, :, :], ALU.mult).then_inc(gated.sem, 1)
                dve.wait_ge(gated.sem, gated.at(c, 7))
                dve.tensor_reduce(total[:, :], chosen[:, :, :], AX.X, ALU.add).then_inc(gated.sem, 1)
                dve.wait_ge(gated.sem, gated.at(c, 8))
                dve.tensor_scalar(total[:, :], total[:, :], TINY, None, ALU.add).then_inc(gated.sem, 1)
                dve.wait_ge(gated.sem, gated.at(c, 9))
                dve.reciprocal(total[:, :], total[:, :]).then_inc(gated.sem, 1)
                dve.wait_ge(gated.sem, gated.at(c, 10))
                dve.scalar_tensor_tensor(gates[:, bass.ds(c * CK, CK), :], chosen[:, :, :], GATE_SCALE,
                                         total[:, :].unsqueeze(2).broadcast_to([P, CK, E]), ALU.mult, ALU.mult
                                         ).then_inc(gated.sem, 1)

            def split(c, n):
                dve.wait_ge(bent.sem, bent.at(c, n + 1))
                dve.wait_ge(up.sem, up.at(c, 2 * n + 2))
                one = hid_one[n % 2]
                hi, lo = hid[n % 2]
                dve.tensor_tensor(one[:, :], ps_u[n % 2][:, :], bent_out[n % 2][:, :], ALU.mult
                                  ).then_inc(hid_cut.sem, 1)
                dve.wait_ge(hid_cut.sem, hid_cut.at(c, 3 * n + 1))
                dve.wait_ge(down.sem, down.at(c, max(n - 1, 0)))
                dve.tensor_copy(hi[:, :], one[:, :]).then_inc(hid_cut.sem, 1)
                dve.wait_ge(hid_cut.sem, hid_cut.at(c, 3 * n + 2))
                dve.tensor_tensor(lo[:, :], one[:, :], hi[:, :].bitcast(F32), ALU.subtract).then_inc(hid_cut.sem, 1)

            def store(c, n):
                if n == 0:
                    dve.wait_ge(gated.sem, gated.at(c, 11))
                if n < E:
                    dve.wait_ge(down.sem, down.at(c, n + 1))
                    for i in range(CK):
                        t = c * CK + i
                        last = dve.scalar_tensor_tensor(kit.x[:, t, :], ps_y[:, i, :], gates[:, t, n:n + 1],
                                                        kit.x[:, t, :], ALU.mult, ALU.add)
                else:
                    dve.wait_ge(down.sem, down.at(c, E + 1))
                    x = kit.x[:, bass.ds(c * CK, CK), :]
                    last = dve.tensor_tensor(x, ps_y[:, :, :], x, ALU.add)
                last.then_inc(stored.sem, 1)

            def body(c, last):
                for n in range(1, units):
                    split(c, n)
                    if n <= E:
                        store(c, n - 1)
                    if not last and n == 2:
                        vary(c + 1)
                    if not last and n == 4:
                        norm(c + 1)
                if not last:
                    flip_out(c + 1)
                store(c, E)
                if not last:
                    split(c + 1, 0)
                    gate(c + 1)

            vary(0)
            norm(0)
            flip_out(0)
            split(0, 0)
            gate(0)
            with dve.Fori(0, NCH - 1) as c:
                body(c, False)
            body(NCH - 1, True)

        @block.tensor
        def _(pe):
            def flip(c):
                pe.wait_ge(normed.sem, normed.at(c, 1))
                pe.wait_ge(grown.sem, grown.at(c, 0))
                for t in range(CT):
                    for i in range(CK):
                        last = pe.transpose(ps_t[:, t, i * P:(i + 1) * P], n_in[:, i, t * P:(t + 1) * P], kit.ident[:, :])
                last.then_inc(flipped.sem, 1)

            def judge(c):
                pe.wait_ge(cut.sem, cut.at(c, 1))
                for i in range(CK):
                    for t in range(CT):
                        last = product(pe, ps_t[:, 0, i * E:(i + 1) * E],
                                       [x[:, t, i * P:(i + 1) * P] for x in x_in],
                                       kit.weights(w_score + t * E, E), t == 0, t == CT - 1)
                last.then_inc(scored.sem, 1)

            def rise(c, n):
                pe.wait_ge(bent.sem, bent.at(c, n - 1))
                for t in range(CT):
                    w = w_gate + t * E * P + n * P if n < E else s_gate + t * C + (n - E) * P
                    last = product(pe, ps_g[n % 2][:, :], kit.weights(w, P), [x[:, t, :] for x in x_in],
                                   t == 0, t == CT - 1)
                last.then_inc(up.sem, 1)
                pe.wait_ge(hid_cut.sem, hid_cut.at(c, 3 * n - 5))
                for t in range(CT):
                    w = w_up + t * E * P + n * P if n < E else s_up + t * C + (n - E) * P
                    last = product(pe, ps_u[n % 2][:, :], kit.weights(w, P), [x[:, t, :] for x in x_in],
                                   t == 0, t == CT - 1)
                last.then_inc(up.sem, 1)

            def fall(c, n):
                last_unit = n if n < E else units - 1
                pe.wait_ge(hid_cut.sem, hid_cut.at(c, 3 * last_unit + 3))
                pe.wait_ge(stored.sem, stored.at(c, n))
                for i in range(CK):
                    for t in range(1 if n < E else CT):
                        w = w_down + n * C if n < E else s_down + t * C
                        last = product(pe, ps_y[:, i, :], [h[:, i * P:(i + 1) * P] for h in hid[(n + t) % 2]],
                                       kit.weights(w, C), t == 0, n < E or t == CT - 1)
                last.then_inc(down.sem, 1)

            def body(c, last):
                for n in range(1, units):
                    rise(c, n)
                    if n <= E:
                        fall(c, n - 1)
                    if not last and n == 5:
                        flip(c + 1)
                fall(c, E)
                if not last:
                    judge(c + 1)
                    rise(c + 1, 0)

            flip(0)
            judge(0)
            rise(0, 0)
            with pe.Fori(0, NCH - 1) as c:
                body(c, False)
            body(NCH - 1, True)

    fetch.end()
    for s_ in (varied, rooted, normed, flipped, shaped, cut, scored, grown, gated, up, bent, hid_cut, down, stored):
        s_.end(NCH)


def wide_attention(kit, own, w_ternary):
    nc, dram, tag = kit.nc, kit.dram, "wide"
    w_q, w_k, w_v = own, own + CT * C, own + CT * C + C

    with ExitStack() as ctx:
        work = Space(nc, tag, kit.late)
        kv_in = [work.take(f"kv_in_{p}", [P, S], F32R) for p in ("hi", "lo")]
        n_in = work.take("n_in", [P, TB, C])
        q_in = [work.take(f"q_in_{p}", [P, CT, S], F32R) for p in ("hi", "lo")]
        q = [work.take(f"q_{p}", [P, CT, S], F32R) for p in ("hi", "lo")]
        k = [work.take(f"k_{p}", [P, CT, S], F32R) for p in ("hi", "lo")]
        v_one = work.take("v_one", [P, TB, C])
        v = [work.take(f"v_{p}", [P, TB, C], F32R) for p in ("hi", "lo")]
        probs = work.take("probs", [P, TB, S])
        turned = [work.take(f"turned_{p}", [P, TB, S], F32R) for p in ("hi", "lo")]
        top = work.take("top", [P, TB])
        sums = work.take("sums", [P, TB])
        inv = work.take("inv", [P, TB])
        stats = work.take("stats", [P, TB, 6])
        mean_var = work.take("mean_var", [P, TB, 2])
        spread = work.take("spread", [P, TB])
        rstd = work.take("rstd", [P, TB])
        v_bias = work.take("v_bias", [P, C])
        ps_t = ctx.enter_context(nc.psum_tensor(f"{tag}_ps_t", [P, CT, S], F32))
        ps_qk = [ctx.enter_context(nc.psum_tensor(f"{tag}_ps_{n}", [P, CT, S], F32)) for n in "qk"]
        ps_v = ctx.enter_context(nc.psum_tensor(f"{tag}_ps_v", [P, TB, C], F32))
        ps_s = ctx.enter_context(nc.psum_tensor(f"{tag}_ps_s", [P, TB, S], F32))
        ps_p = ctx.enter_context(nc.psum_tensor(f"{tag}_ps_p", [P, TB, S], F32))
        ps_o = ctx.enter_context(nc.psum_tensor(f"{tag}_ps_o", [P, TB, C], F32))

        rows_in = kit.counter("rows_in")
        w_in = kit.counter("x_in")
        varied = kit.counter("varied")
        rooted = kit.counter("rooted")
        normed = kit.counter("normed")
        flipped = kit.counter("flipped")
        shaped = kit.counter("shaped")
        cut = kit.counter("cut")
        projected = kit.counter("projected")
        q_high = kit.counter("q_high")
        qk_cut = kit.counter("qk_cut")
        v_made = kit.counter("v_made")
        scored = kit.counter("scored")
        maxed = kit.counter("maxed")
        exped = kit.counter("exped")
        turned_out = kit.counter("turned_out")
        leaf_high = kit.counter("leaf_high")
        leaf_low = kit.counter("leaf_low")
        weighed = kit.counter("weighed")
        mended = kit.counter("mended")
        stored = kit.counter("stored")
        for s_ in (rows_in, w_in, rooted, normed, flipped, shaped, cut, v_made, scored, maxed, exped, turned_out,
                   leaf_high, leaf_low, weighed, mended, stored):
            s_.begin(1)
        shaped.begin(2)
        cut.begin(2)
        varied.begin(3)
        for s_ in (projected, q_high, qk_cut):
            s_.begin(3)
        block = ctx.enter_context(nc.Block())

        @block.sync
        def _(sp):
            sp.dma_start(v_bias[:, :], dram["rows"]["L3_bv"].broadcast_to([P, C])).then_inc(rows_in.sem, 16)
            sp.dma_start(w_ternary[:, :], dram["w_ternary"]).then_inc(w_in.sem, 16)
            sp.wait_ge(w_in.sem, w_in.at(0, 1))

        @block.gpsimd
        def _(pool):
            with pool.Fori(0, B) as b:
                pool.wait_ge(varied.sem, varied.at(b, 3))
                pool.tensor_tensor(rstd[:, :], spread[:, :], kit.power[:, 0:TB], ALU.pow).then_inc(rooted.sem, 1)

        @block.scalar
        def _(act):
            def flip_out(b):
                act.wait_ge(flipped.sem, flipped.at(b, 1))
                act.wait_ge(projected.sem, projected.at(b, 0))
                act.activation(q_in[0][:, :, :], ps_t[:, :, :], ACT.Identity).then_inc(shaped.sem, 1)
                act.activation(kv_in[0][:, :], kit.ctx_t[:, bass.ds(b * S, S)], ACT.Identity).then_inc(shaped.sem, 1)

            def high(b):
                for n, to in enumerate((q, k)):
                    act.wait_ge(projected.sem, projected.at(b, n + 1))
                    act.wait_ge(scored.sem, scored.at(b, 0))
                    for m in range(CT):
                        last = act.activation(to[0][:, m, :], ps_qk[n][:, m, :], ACT.Identity,
                                              bias=kit.column(("L3_bq", "L3_bk")[n], m))
                    last.then_inc(q_high.sem, 1)
                act.wait_ge(v_made.sem, v_made.at(b, 1))
                act.wait_ge(weighed.sem, weighed.at(b, 0))
                act.activation(v[0][:, :, :], v_one[:, :, :], ACT.Identity).then_inc(q_high.sem, 1)

            def weigh(b):
                act.wait_ge(maxed.sem, maxed.at(b, 1))
                act.wait_ge(turned_out.sem, turned_out.at(b, 0))
                act.wait_ge(mended.sem, mended.at(b, 0))
                for i in range(TB):
                    last = act.activation(probs[:, i, :], ps_s[:, i, :], ACT.Exp, bias=top[:, i:i + 1],
                                          accum_out=sums[:, i:i + 1])
                last.then_inc(exped.sem, 1)

            def turn_out(b):
                act.wait_ge(turned_out.sem, turned_out.at(b, 1))
                act.wait_ge(weighed.sem, weighed.at(b, 0))
                act.activation(turned[0][:, :, :], ps_p[:, :, :], ACT.Identity).then_inc(leaf_high.sem, 1)

            def body(b, last):
                if not last:
                    flip_out(b + 1)
                weigh(b)
                turn_out(b)
                if not last:
                    high(b + 1)

            flip_out(0)
            high(0)
            with act.Fori(0, B - 1) as b:
                body(b, False)
            body(B - 1, True)

        @block.vector
        def _(dve):
            def vary(b):
                for i in range(TB):
                    last = dve.bn_stats(stats[:, i, :], kit.x[:, b * TB + i, :])
                last.then_inc(varied.sem, 1)
                dve.wait_ge(varied.sem, varied.at(b, 1))
                kit.apart(dve)
                for i in range(TB):
                    last = dve.bn_aggr(mean_var[:, i, :], stats[:, i, :])
                last.then_inc(varied.sem, 1)
                dve.wait_ge(varied.sem, varied.at(b, 2))
                dve.tensor_scalar(spread[:, :], mean_var[:, :, 1], EPS, None, ALU.add).then_inc(varied.sem, 1)

            def norm(b):
                dve.wait_ge(rooted.sem, rooted.at(b, 1))
                dve.wait_ge(flipped.sem, flipped.at(b, 0))
                for i in range(TB):
                    last = dve.tensor_scalar(n_in[:, i, :], kit.x[:, b * TB + i, :], mean_var[:, i, 0:1],
                                             rstd[:, i:i + 1], ALU.subtract, ALU.mult)
                last.then_inc(normed.sem, 1)

            def flip_out(b):
                dve.wait_ge(shaped.sem, shaped.at(b, 1))
                dve.tensor_tensor(q_in[1][:, :, :], ps_t[:, :, :], q_in[0][:, :, :].bitcast(F32), ALU.subtract
                                  ).then_inc(cut.sem, 1)
                dve.wait_ge(shaped.sem, shaped.at(b, 2))
                dve.tensor_tensor(kv_in[1][:, :], kit.ctx_t[:, bass.ds(b * S, S)], kv_in[0][:, :].bitcast(F32),
                                  ALU.subtract).then_inc(cut.sem, 1)

            def low(b):
                for n, to in enumerate((q, k)):
                    dve.wait_ge(q_high.sem, q_high.at(b, n + 1))
                    for m in range(CT):
                        last = dve.scalar_tensor_tensor(to[1][:, m, :], ps_qk[n][:, m, :],
                                                        kit.column(("L3_bq", "L3_bk")[n], m),
                                                        to[0][:, m, :].bitcast(F32), ALU.add, ALU.subtract)
                    last.then_inc(qk_cut.sem, 1)
                dve.wait_ge(projected.sem, projected.at(b, 3))
                for i in range(TB):
                    last = dve.tensor_tensor(v_one[:, i, :], ps_v[:, i, :], v_bias[:, :], ALU.add)
                last.then_inc(v_made.sem, 1)
                dve.wait_ge(q_high.sem, q_high.at(b, 3))
                dve.tensor_tensor(v[1][:, :, :], v_one[:, :, :], v[0][:, :, :].bitcast(F32), ALU.subtract
                                  ).then_inc(qk_cut.sem, 1)

            def tops(b):
                dve.wait_ge(scored.sem, scored.at(b, 1))
                dve.wait_ge(exped.sem, exped.at(b, 0))
                dve.tensor_reduce(top[:, :], ps_s[:, :, :], AX.X, ALU.max, negate=True).then_inc(maxed.sem, 1)

            def turn_out(b):
                dve.wait_ge(leaf_high.sem, leaf_high.at(b, 1))
                dve.tensor_tensor(turned[1][:, :, :], ps_p[:, :, :], turned[0][:, :, :].bitcast(F32), ALU.subtract
                                  ).then_inc(leaf_low.sem, 1)

            def store(b):
                dve.wait_ge(exped.sem, exped.at(b, 1))
                dve.reciprocal(inv[:, :], sums[:, :]).then_inc(mended.sem, 1)
                dve.wait_ge(mended.sem, mended.at(b, 1))
                dve.wait_ge(weighed.sem, weighed.at(b, 1))
                for i in range(TB):
                    t = kit.x[:, b * TB + i, :]
                    last = dve.scalar_tensor_tensor(t, ps_o[:, i, :], inv[:, i:i + 1], t, ALU.mult, ALU.add)
                last.then_inc(stored.sem, 1)

            def body(b, more):
                tops(b)
                if more >= 1:
                    flip_out(b + 1)
                turn_out(b)
                if more >= 1:
                    low(b + 1)
                if more >= 2:
                    vary(b + 2)
                    norm(b + 2)
                store(b)

            vary(0)
            norm(0)
            dve.wait_ge(rows_in.sem, rows_in.at(0, 1))
            flip_out(0)
            low(0)
            vary(1)
            norm(1)
            with dve.Fori(0, B - 2) as b:
                body(b, 2)
            body(B - 2, 1)
            body(B - 1, 0)

        @block.tensor
        def _(pe):
            def flip(b):
                pe.wait_ge(normed.sem, normed.at(b, 1))
                pe.wait_ge(cut.sem, cut.at(b, 0))
                for t in range(CT):
                    for i in range(TB):
                        last = pe.transpose(ps_t[:, t, i * P:(i + 1) * P], n_in[:, i, t * P:(t + 1) * P], kit.ident[:, :])
                last.then_inc(flipped.sem, 1)

            def project(b):
                pe.wait_ge(cut.sem, cut.at(b, 2))
                pe.wait_ge(qk_cut.sem, qk_cut.at(b, 0))
                for m in range(CT):
                    for t in range(CT):
                        last = product(pe, ps_qk[0][:, m, :], kit.weights(w_q + t * C + m * P, P),
                                       [x[:, t, :] for x in q_in], t == 0, t == CT - 1)
                last.then_inc(projected.sem, 1)
                for m in range(CT):
                    last = product(pe, ps_qk[1][:, m, :], kit.weights(w_k + m * P, P),
                                   [x[:, :] for x in kv_in], True, True)
                last.then_inc(projected.sem, 1)
                for i in range(TB):
                    last = product(pe, ps_v[:, i, :], [x[:, i * P:(i + 1) * P] for x in kv_in],
                                   kit.weights(w_v, C), True, True)
                last.then_inc(projected.sem, 1)

            def score(b):
                pe.wait_ge(qk_cut.sem, qk_cut.at(b, 2))
                pe.wait_ge(exped.sem, exped.at(b, 0))
                for i in range(TB):
                    for m in range(CT):
                        last = product(pe, ps_s[:, i, :], [x[:, m, i * P:(i + 1) * P] for x in q],
                                       [x[:, m, :] for x in k], m == 0, m == CT - 1)
                last.then_inc(scored.sem, 1)

            def turn(b):
                pe.wait_ge(exped.sem, exped.at(b, 1))
                pe.wait_ge(leaf_low.sem, leaf_low.at(b, 0))
                for t in range(TB):
                    for i in range(TB):
                        last = pe.transpose(ps_p[:, t, i * P:(i + 1) * P], probs[:, i, t * P:(t + 1) * P], kit.ident[:, :])
                last.then_inc(turned_out.sem, 1)

            def weigh(b):
                pe.wait_ge(leaf_low.sem, leaf_low.at(b, 1))
                pe.wait_ge(qk_cut.sem, qk_cut.at(b, 3))
                pe.wait_ge(stored.sem, stored.at(b, 0))
                for i in range(TB):
                    for t in range(TB):
                        last = product(pe, ps_o[:, i, :], [x[:, t, i * P:(i + 1) * P] for x in turned],
                                       [x[:, t, :] for x in v], t == 0, t == TB - 1)
                last.then_inc(weighed.sem, 1)

            def body(b, last):
                score(b)
                if not last:
                    flip(b + 1)
                turn(b)
                if not last:
                    project(b + 1)
                weigh(b)

            flip(0)
            project(0)
            with pe.Fori(0, B - 1) as b:
                body(b, False)
            body(B - 1, True)

    for s_ in (rows_in, w_in):
        s_.end(1)
    for s_ in (varied, rooted, normed, flipped, shaped, cut, projected, q_high, qk_cut, v_made, scored, maxed, exped,
               turned_out, leaf_high, leaf_low, weighed, mended, stored):
        s_.end(B)


def ternary(kit, w_raw):
    nc, tag = kit.nc, "ternary"
    pairs = NT // 2
    mat = CT * FF
    mats = 3
    half = FF // 2

    with ExitStack() as ctx:
        work = Space(nc, tag, [*kit.late, *kit.slot_ranges[2]])
        w = work.take("w", [P, mats * mat], BF16)
        ident = work.take("ident", [P, P], BF16)
        ones = work.take("ones", [P, P])
        minus_round = work.take("minus_round", [P, 1])
        magnitude = work.take("magnitude", [P, mats])
        unit = work.take("unit", [P, mats])
        unit_level = work.take("unit_level", [P, mats])
        w_scale = work.take("w_scale", [P, mats])
        n_in = work.take("n_in", [P, 2, C])
        n_int = work.take("n_int", [P, 2, C], BF16)
        x_t = work.take("x_t", [P, CT, 2 * P], BF16)
        most = work.take("most", [P, 2])
        scale = work.take("scale", [P, 2])
        up_unit = [work.take(f"up_unit{k}", [P, 2]) for k in range(2)]
        bent_out = [work.take(f"bent_out{i}", [P, FF]) for i in range(2)]
        hid = [work.take(f"hid{i}", [P, FF]) for i in range(2)]
        hid_int = [work.take(f"hid_int{i}", [P, FF], BF16) for i in range(2)]
        hid_t = work.take("hid_t", [P, FT, P], BF16)
        h_most = work.take("h_most", [P, 2])
        h_scale = work.take("h_scale", [P, 2])
        y_unit = work.take("y_unit", [P, 2])
        stats = work.take("stats", [P, 2, 6])
        mean_var = work.take("mean_var", [P, 2, 2])
        spread = work.take("spread", [P, 2])
        rstd = work.take("rstd", [P, 2])
        ps_g = ctx.enter_context(nc.psum_tensor(f"{tag}_ps_g", [P, FF], F32))
        ps_u = ctx.enter_context(nc.psum_tensor(f"{tag}_ps_u", [P, FF], F32))
        ps_h = ctx.enter_context(nc.psum_tensor(f"{tag}_ps_h", [P, FT, P], BF16))
        ps_t = ctx.enter_context(nc.psum_tensor(f"{tag}_ps_t", [P, CT, 4 * P], BF16))
        ps_y = ctx.enter_context(nc.psum_tensor(f"{tag}_ps_y", [P, 512], F32))

        zeroed = kit.counter("set_up")
        weighed = kit.counter("weighed")
        planted = kit.counter("planted")
        shifted = kit.counter("shifted")
        varied = kit.counter("varied")
        rooted = kit.counter("rooted")
        normed = kit.counter("normed")
        flipped = kit.counter("flipped")
        shaped = kit.counter("shaped")
        up = kit.counter("up")
        bent = kit.counter("bent")
        hid_cut = kit.counter("hid_cut")
        valued = kit.counter("valued")
        turned_out = kit.counter("turned_out")
        leaf_high = kit.counter("leaf_high")
        gathered = kit.counter("gathered")
        stored = kit.counter("stored")
        zeroed.begin(3)
        weighed.begin(2)
        planted.begin(3 + 2 * mats)
        shifted.begin(mats)
        varied.begin(3)
        for s_ in (rooted, flipped, shaped):
            s_.begin(1)
        normed.begin(9)
        up.begin(4)
        for s_ in (bent, valued, turned_out, leaf_high, gathered, stored):
            s_.begin(2)
        steps = 8
        hid_cut.begin(2 * steps)
        block = ctx.enter_context(nc.Block())

        @block.gpsimd
        def _(pool):
            pool.memset(ones[:, :], 1.0).then_inc(zeroed.sem, 1)
            pool.memset(minus_round[:, :], -ROUND).then_inc(zeroed.sem, 1)
            pool.tensor_copy(ident[:, :], kit.ident[:, :]).then_inc(zeroed.sem, 1)
            with pool.Fori(0, pairs) as p:
                pool.wait_ge(varied.sem, varied.at(p, 3))
                pool.tensor_tensor(rstd[:, :], spread[:, :], kit.power[:, 0:2], ALU.pow).then_inc(rooted.sem, 1)

        @block.scalar
        def _(act):
            for k in range(mats):
                last = act.activation(w[:, k * mat:(k + 1) * mat], w_raw[:, k * mat:(k + 1) * mat], ACT.Abs,
                                      accum_out=magnitude[:, k:k + 1])
            last.then_inc(weighed.sem, 1)

            def flip_out(p):
                act.wait_ge(flipped.sem, flipped.at(p, 1))
                act.wait_ge(up.sem, up.at(p, 0))
                act.activation(x_t[:, :, :], ps_t[:, :, 0:2 * P], ACT.Identity).then_inc(shaped.sem, 1)

            def bend(p, i):
                act.wait_ge(up.sem, up.at(p, 2 * i + 1))
                act.wait_ge(normed.sem, normed.at(p, 9))
                act.wait_ge(hid_cut.sem, hid_cut.at(p, steps * (i - 2) + 1))
                act.activation(bent_out[i][:, :], ps_g[:, :], ACT.Silu, scale=up_unit[0][:, i:i + 1]
                               ).then_inc(bent.sem, 1)

            def whole(p, i):
                act.wait_ge(hid_cut.sem, hid_cut.at(p, steps * (i + 1)))
                act.wait_ge(turned_out.sem, turned_out.at(p, i - 1))
                act.activation(hid_int[i][:, :], hid[i][:, :], ACT.Identity, bias=minus_round[:, :]
                               ).then_inc(valued.sem, 1)

            def turn_out(p, i):
                act.wait_ge(turned_out.sem, turned_out.at(p, i + 1))
                act.wait_ge(gathered.sem, gathered.at(p, i))
                act.activation(hid_t[:, :, :], ps_h[:, :, :], ACT.Identity).then_inc(leaf_high.sem, 1)

            def body(p, last):
                if not last:
                    flip_out(p + 1)
                turn_out(p, 0)
                if not last:
                    bend(p + 1, 0)
                turn_out(p, 1)
                if not last:
                    whole(p + 1, 0)
                    bend(p + 1, 1)
                    whole(p + 1, 1)

            act.wait_ge(zeroed.sem, zeroed.at(0, 3))
            for k in range(mats):
                act.wait_ge(planted.sem, planted.at(0, 3 + 2 * (k + 1)))
                act.activation(w[:, k * mat:(k + 1) * mat], w_raw[:, k * mat:(k + 1) * mat], ACT.Identity,
                               bias=minus_round[:, :]).then_inc(shifted.sem, 1)
            flip_out(0)
            bend(0, 0)
            whole(0, 0)
            bend(0, 1)
            whole(0, 1)
            with act.Fori(0, pairs - 1) as p:
                body(p, False)
            body(pairs - 1, True)

        @block.vector
        def _(dve):
            def front(p):
                for i in range(2):
                    last = dve.bn_stats(stats[:, i, :], kit.x[:, p * 2 + i, :])
                last.then_inc(varied.sem, 1)
                dve.wait_ge(varied.sem, varied.at(p, 1))
                kit.apart(dve)
                for i in range(2):
                    last = dve.bn_aggr(mean_var[:, i, :], stats[:, i, :])
                last.then_inc(varied.sem, 1)
                dve.wait_ge(varied.sem, varied.at(p, 2))
                dve.tensor_scalar(spread[:, :], mean_var[:, :, 1], EPS, None, ALU.add).then_inc(varied.sem, 1)
                dve.wait_ge(rooted.sem, rooted.at(p, 1))
                for i in range(2):
                    last = dve.tensor_scalar(n_in[:, i, :], kit.x[:, p * 2 + i, :], mean_var[:, i, 0:1],
                                             rstd[:, i:i + 1], ALU.subtract, ALU.mult)
                last.then_inc(normed.sem, 1)
                dve.wait_ge(normed.sem, normed.at(p, 1))
                dve.tensor_reduce(most[:, :], n_in[:, :, :], AX.X, ALU.max, apply_absolute_value=True
                                  ).then_inc(normed.sem, 1)
                dve.wait_ge(normed.sem, normed.at(p, 2))
                dve.tensor_scalar(most[:, :], most[:, :], FLOOR, None, ALU.max).then_inc(normed.sem, 1)
                dve.wait_ge(normed.sem, normed.at(p, 3))
                dve.reciprocal(scale[:, :], most[:, :]).then_inc(normed.sem, 1)
                dve.wait_ge(normed.sem, normed.at(p, 4))
                dve.tensor_scalar(scale[:, :], scale[:, :], LEVELS, None, ALU.mult).then_inc(normed.sem, 1)
                dve.wait_ge(normed.sem, normed.at(p, 5))
                for i in range(2):
                    last = dve.tensor_scalar(n_in[:, i, :], n_in[:, i, :], scale[:, i:i + 1], LEVELS, ALU.mult, ALU.min)
                last.then_inc(normed.sem, 1)
                dve.wait_ge(normed.sem, normed.at(p, 6))
                dve.tensor_scalar(n_in[:, :, :], n_in[:, :, :], -LEVELS - 1, ROUND, ALU.max, ALU.add
                                  ).then_inc(normed.sem, 1)
                dve.wait_ge(normed.sem, normed.at(p, 7))
                dve.wait_ge(flipped.sem, flipped.at(p, 0))
                dve.tensor_scalar(n_int[:, :, :], n_in[:, :, :], ROUND, None, ALU.subtract).then_inc(normed.sem, 1)

            def units(p):
                dve.wait_ge(bent.sem, bent.at(p, 0))
                dve.wait_ge(planted.sem, planted.at(0, 3))
                dve.tensor_scalar(up_unit[0][:, :], most[:, :], unit_level[:, 0:1], None, ALU.mult)
                dve.tensor_scalar(up_unit[1][:, :], most[:, :], unit_level[:, 1:2], None, ALU.mult
                                  ).then_inc(normed.sem, 1)

            def hide(p, i):
                k = steps * i
                h, one = hid[i][:, :], slice(i, i + 1)
                dve.wait_ge(normed.sem, normed.at(p, 9))
                dve.wait_ge(up.sem, up.at(p, 2 * i + 2))
                dve.wait_ge(bent.sem, bent.at(p, i + 1))
                dve.wait_ge(valued.sem, valued.at(p, i - 1))
                dve.scalar_tensor_tensor(h, ps_u[:, :], up_unit[1][:, one], bent_out[i][:, :], ALU.mult, ALU.mult
                                         ).then_inc(hid_cut.sem, 1)
                dve.wait_ge(hid_cut.sem, hid_cut.at(p, k + 1))
                dve.tensor_reduce(h_most[:, one], h, AX.X, ALU.max, apply_absolute_value=True).then_inc(hid_cut.sem, 1)
                dve.wait_ge(hid_cut.sem, hid_cut.at(p, k + 2))
                dve.tensor_scalar(h_most[:, one], h_most[:, one], FLOOR, None, ALU.max).then_inc(hid_cut.sem, 1)
                dve.wait_ge(hid_cut.sem, hid_cut.at(p, k + 3))
                dve.reciprocal(h_scale[:, one], h_most[:, one]).then_inc(hid_cut.sem, 1)
                dve.wait_ge(hid_cut.sem, hid_cut.at(p, k + 4))
                dve.tensor_scalar(h_scale[:, one], h_scale[:, one], LEVELS, None, ALU.mult).then_inc(hid_cut.sem, 1)
                dve.wait_ge(hid_cut.sem, hid_cut.at(p, k + 5))
                dve.tensor_scalar(h, h, h_scale[:, one], LEVELS, ALU.mult, ALU.min).then_inc(hid_cut.sem, 1)
                dve.wait_ge(hid_cut.sem, hid_cut.at(p, k + 6))
                dve.wait_ge(stored.sem, stored.at(p, i - 1))
                dve.tensor_tensor(y_unit[:, one], h_most[:, one], unit_level[:, 2:3], ALU.mult).then_inc(hid_cut.sem, 1)
                dve.tensor_scalar(h, h, -LEVELS - 1, ROUND, ALU.max, ALU.add).then_inc(hid_cut.sem, 1)

            def store(p, i):
                dve.wait_ge(gathered.sem, gathered.at(p, i + 1))
                t = kit.x[:, p * 2 + i, :]
                dve.scalar_tensor_tensor(t, ps_y[:, 0:C], y_unit[:, i:i + 1], t, ALU.mult, ALU.add
                                         ).then_inc(stored.sem, 1)

            def body(p, last):
                if not last:
                    front(p + 1)
                    units(p + 1)
                store(p, 0)
                if not last:
                    hide(p + 1, 0)
                store(p, 1)
                if not last:
                    hide(p + 1, 1)

            dve.wait_ge(zeroed.sem, zeroed.at(0, 3))
            front(0)
            dve.wait_ge(weighed.sem, weighed.at(0, 2))
            dve.tensor_scalar(unit[:, :], ps_y[:, 0:mats], 1.0 / (P * mat), FLOOR, ALU.mult, ALU.max
                              ).then_inc(planted.sem, 1)
            dve.wait_ge(planted.sem, planted.at(0, 1))
            dve.reciprocal(w_scale[:, :], unit[:, :]).then_inc(planted.sem, 1)
            dve.tensor_scalar(unit_level[:, :], unit[:, :], 1.0 / LEVELS, None, ALU.mult).then_inc(planted.sem, 1)
            dve.wait_ge(planted.sem, planted.at(0, 3))
            for k in range(mats):
                m = w_raw[:, k * mat:(k + 1) * mat]
                dve.tensor_scalar(m, m, w_scale[:, k:k + 1], 1.0, ALU.mult, ALU.min).then_inc(planted.sem, 1)
                dve.wait_ge(planted.sem, planted.at(0, 3 + 2 * k + 1))
                dve.tensor_scalar(m, m, -1.0, ROUND, ALU.max, ALU.add).then_inc(planted.sem, 1)
            units(0)
            hide(0, 0)
            hide(0, 1)
            with dve.Fori(0, pairs - 1) as p:
                body(p, False)
            body(pairs - 1, True)

        @block.tensor
        def _(pe):
            def flip(p):
                pe.wait_ge(normed.sem, normed.at(p, 8))
                pe.wait_ge(shaped.sem, shaped.at(p, 0))
                for t in range(CT):
                    for i in range(2):
                        last = pe.transpose(ps_t[:, t, i * P:(i + 1) * P], n_int[:, i, t * P:(t + 1) * P], ident[:, :])
                last.then_inc(flipped.sem, 1)

            def rise(p, i):
                if i == 0:
                    pe.wait_ge(shaped.sem, shaped.at(p, 1))
                for k, out in enumerate((ps_g, ps_u)):
                    if k:
                        pe.wait_ge(hid_cut.sem, hid_cut.at(p, steps * (i - 1) + 1))
                    else:
                        pe.wait_ge(bent.sem, bent.at(p, i))
                    for n in range(2):
                        for t in range(CT):
                            at = k * mat + t * FF + n * half
                            last = pe.matmul(out[:, n * half:(n + 1) * half], x_t[:, t, i * P:(i + 1) * P],
                                             w[:, at:at + half], start=t == 0, stop=t == CT - 1)
                    last.then_inc(up.sem, 1)

            def turn(p, i):
                pe.wait_ge(valued.sem, valued.at(p, i + 1))
                pe.wait_ge(leaf_high.sem, leaf_high.at(p, i))
                for f in range(FT):
                    last = pe.transpose(ps_h[:, f, :], hid_int[i][:, f * P:(f + 1) * P], ident[:, :])
                last.then_inc(turned_out.sem, 1)

            def gather(p, i):
                pe.wait_ge(leaf_high.sem, leaf_high.at(p, i + 1))
                pe.wait_ge(stored.sem, stored.at(p, i))
                for f in range(FT):
                    at = 2 * mat + f * C
                    last = pe.matmul(ps_y[:, 0:C], hid_t[:, f, :], w[:, at:at + C], start=f == 0, stop=f == FT - 1)
                last.then_inc(gathered.sem, 1)

            def body(p, last):
                if not last:
                    flip(p + 1)
                for i in range(2):
                    turn(p, i)
                    if not last:
                        rise(p + 1, i)
                    gather(p, i)

            pe.wait_ge(zeroed.sem, zeroed.at(0, 3))
            pe.wait_ge(weighed.sem, weighed.at(0, 1))
            pe.matmul(ps_y[:, 0:mats], ones[:, :], magnitude[:, :], start=True, stop=True).then_inc(weighed.sem, 1)
            flip(0)
            pe.wait_ge(shifted.sem, shifted.at(0, mats))
            pe.wait_ge(planted.sem, planted.at(0, 1))
            rise(0, 0)
            rise(0, 1)
            with pe.Fori(0, pairs - 1) as p:
                body(p, False)
            body(pairs - 1, True)

    for s_ in (zeroed, weighed, planted, shifted):
        s_.end(1)
    for s_ in (varied, rooted, normed, flipped, shaped, up, bent, hid_cut, valued, turned_out, leaf_high, gathered,
               stored):
        s_.end(pairs)


ROWS = ("ln1_g ln1_b ln2_g ln2_b a1_li1_b a1_li3_b a2_li1_b a2_li3_b L2_bv L2_bo L3_bv").split()
COLS = {"a1_lnx_g": 2, "a1_lnx_b": 2, "a1_lny_g": 2, "a1_lny_b": 2, "a1_ln3_g": 2, "a1_ln3_b": 2, "a1_li2_b": 8,
        "a2_lnx_g": 2, "a2_lnx_b": 2, "a2_lny_g": 1, "a2_lny_b": 1, "a2_ln3_g": 2, "a2_ln3_b": 2, "a2_li2_b": 8,
        "rb1": 8, "b1": 64, "L2_bq": 2, "L2_bk": 2, "L3_bq": 2, "L3_bk": 2}


def program(nc, dram):
    col_at, at = {}, 0
    for name, n in COLS.items():
        col_at[name] = at
        at += n
    dram["col_at"] = col_at
    dram["rows"] = {name: dram["rows"][n:n + 1, :] for n, name in enumerate(ROWS)}
    with ExitStack() as ctx:
        kit = Kit(nc, ctx, dram)
        opening(kit)
        attention(kit, "a1", 32, True, "self", 32 ** -0.5, 0, (dram["w_f1"], SLOT, SLOT), ("a1_lnx_g", "a1_lnx_b"),
                  ("a1_lny_g", "a1_lny_b"), out_bias="a1_li1_b", free=kit.slot_ranges[2])
        feed_forward(kit, "fa1", SLOT, (dram["w_a2"], 2 * SLOT, 3072), False, free=())
        attention(kit, "a2", 32, False, "norm", 32 ** -0.5, 2 * SLOT, (dram["w_f2"], 0, SLOT), ("a2_lnx_g", "a2_lnx_b"),
                  ("a2_lny_g", "a2_lny_b"), out_bias="a2_li1_b", free=kit.slot_ranges[1])
        feed_forward(kit, "fa2", 0, (dram["w_router"], SLOT, 2112), True)
        spare = Space(nc, "late", kit.late)
        x_all = [spare.take(f"x_all_{p}", [P, CT, B * S], F32R) for p in ("hi", "lo")]
        gates = spare.take("gates", [P, NT, E])
        kit.rest = spare.free
        router(kit, SLOT, (dram["w_experts"][0], 2 * SLOT, SLOT), x_all, gates)
        experts(kit, (2 * SLOT, 0), dram["w_experts"], x_all, gates)
        attention(kit, "b1", 16, False, "raw", 16 ** -0.5, 2 * SLOT, (dram["w_tree"], 0, 2 * SLOT))
        tree(kit, 0, (dram["w_b2"], 2 * SLOT, 2048))
        attention(kit, "b2", 16, False, "raw", 16 ** -0.5, 2 * SLOT, (dram["w_swiglu"], 0, SWIGLU), q_bias="L2_bq",
                  k_bias="L2_bk", v_bias="L2_bv", out_bias="L2_bo")
        swiglu(kit, 0, (dram["w_b3"], 2 * SLOT, 1024))
        w_ternary = nc.alloc_sbuf_tensor_at("w_ternary", [P, 3 * CT * FF], F32, offset=kit.slot_ranges[0][0][0])
        wide_attention(kit, 2 * SLOT, w_ternary)
        ternary(kit, w_ternary)
        closing(kit)


def closing(kit):
    with kit.nc.Block() as block:
        done = kit.counter("x_in")
        done.begin(1)

        @block.sync
        def _(sp):
            sp.dma_start(kit.dram["out"], kit.x[:, :, :]).then_inc(done.sem, 16)
            sp.wait_ge(done.sem, done.at(0, 1))
        done.end(1)


def tiles(w):
    k, m = w.shape
    return w.reshape(k // P, P, m).transpose(1, 0, 2).reshape(P, -1)


def widen(w, n):
    out = np.zeros((w.shape[0], n), w.dtype)
    out[:, :w.shape[1]] = w
    return out


def attention_weights(wq, wk, wv, wo):
    rows = np.zeros((HEADS, 32, C), wo.dtype)
    rows[:, :C // HEADS] = wo.reshape(HEADS, C // HEADS, C)
    return np.concatenate([tiles(wq), tiles(wk), tiles(wv), tiles(rows.reshape(HEADS * 32, C))], 1)


def layout(i):
    i = {k: np.asarray(v) for k, v in i.items()}
    heads = lambda w: w.transpose(1, 0, 2).reshape(w.shape[1], -1)
    side = lambda *ws: np.ascontiguousarray(np.concatenate(ws, 1))
    out = {}
    out["x"] = np.ascontiguousarray(i["x"].reshape(NT, P, C).transpose(1, 0, 2))
    out["ctx"] = np.ascontiguousarray(i["ctx_512"].reshape(NT, P, CD).transpose(1, 0, 2))
    out["ctx_t"] = np.ascontiguousarray(i["ctx_512"].reshape(B * S, CD).T)
    a1, a2 = "L0_xattn_a1_", "L0_xattn_a2_"
    for n, a in (("1", a1), ("2", a2)):
        out["w_a" + n] = side(*[tiles(heads(i[a + w])) for w in ("wq", "wk", "wv")], tiles(i[a + "li1_w"]))
        out["w_f" + n] = side(tiles(i[a + "li2_w"]), tiles(i[a + "li3_w"]))
    out["w_router"] = side(tiles(i["L0_ffn_rw1"]), tiles(i["L0_ffn_rw2"]))
    w1, w2 = i["L0_ffn_W1"], i["L0_ffn_W2"]
    out["w_experts"] = np.stack([side(tiles(w1[e]), tiles(w2[e])) for e in range(E)] + [widen(attention_weights(
        i["L1_xattn_Wq"].T, i["L1_xattn_Wkv"][:C].T, i["L1_xattn_Wkv"][C:].T, i["L1_xattn_Wo"].T), SLOT)])
    out["w_tree"] = side(tiles(i["L1_ffn_W_in"].T), np.zeros((P, SLOT - CT * NODES), np.float32),
                         tiles(widen(i["L1_ffn_W_out"], TREE_T * P).T))
    out["tree_bias"] = np.ascontiguousarray(i["L1_ffn_b_in"].reshape(1, NODES))
    out["w_b2"] = attention_weights(i["L2_xattn_Wq"], i["L2_xattn_Wk"], i["L2_xattn_Wv"], i["L2_xattn_Wo"])
    flat = lambda w: tiles(w.transpose(2, 0, 1).reshape(w.shape[2], -1))
    out["w_swiglu"] = side(flat(i["L2_ffn_w_gate"]), flat(i["L2_ffn_w_up"]),
                           i["L2_ffn_w_down"].transpose(2, 0, 1).reshape(P, E * C),
                           tiles(i["L2_ffn_ws_gate"].T), tiles(i["L2_ffn_ws_up"].T), tiles(i["L2_ffn_ws_down"].T),
                           tiles(i["L2_ffn_gate_weight"].T))
    out["w_b3"] = side(tiles(i["L3_xattn_Wq"]), tiles(i["L3_xattn_Wk"]), tiles(i["L3_xattn_Wv"]))
    out["w_ternary"] = side(*[tiles(i["L3_ffn_w_" + n].T) for n in ("gate", "up", "down")])
    out["rb2"] = i["L0_ffn_rb2"].reshape(1, E)
    out["b2"] = np.ascontiguousarray(i["L0_ffn_b2"].reshape(1, E * C))
    out["lower"] = np.ascontiguousarray(np.broadcast_to(np.tril(np.ones((E, E), np.float32), -1), (P, E, E)))
    rows = {"ln1_g": "L0_xattn_ln1_g", "ln1_b": "L0_xattn_ln1_b", "ln2_g": "L0_xattn_ln2_g", "ln2_b": "L0_xattn_ln2_b",
            "a1_li1_b": a1 + "li1_b", "a1_li3_b": a1 + "li3_b", "a2_li1_b": a2 + "li1_b", "a2_li3_b": a2 + "li3_b",
            "L2_bv": "L2_xattn_bv", "L2_bo": "L2_xattn_bo", "L3_bv": "L3_xattn_bv"}
    out["rows"] = np.stack([i[rows[n]] for n in ROWS])
    cols = {"rb1": "L0_ffn_rb1", "b1": "L0_ffn_b1", "L2_bq": "L2_xattn_bq", "L2_bk": "L2_xattn_bk",
            "L3_bq": "L3_xattn_bq", "L3_bk": "L3_xattn_bk"}
    out["cols"] = side(*[i[cols.get(n, "L0_xattn_" + n)].reshape(-1, P).T for n in COLS])
    out["ident"] = np.eye(P, dtype=np.float32)
    tri = np.tril(np.ones((P, P), np.float32), -1)
    out["tri"] = np.ascontiguousarray(np.stack([tri, tri], 1))
    return out


def kernel(**inputs):
    import concourse.bacc as bacc
    from concourse.bass_utils import run_bass_kernel_spmd

    arrays = layout(inputs)
    nc = bacc.Bacc("TRN2", target_bir_lowering=False, num_devices=1)
    dram = {name: nc.dram_tensor(name, a.shape, mybir.dt.from_np(a.dtype), kind="ExternalInput").ap()
            for name, a in arrays.items()}
    dram["out"] = nc.dram_tensor("out_0_dram", (P, NT, C), F32, kind="ExternalOutput").ap()
    dram["heads"] = nc.dram_tensor("heads", (2, 4, C, S), F32, kind="Internal").ap()
    program(nc, dram)
    result = run_bass_kernel_spmd(nc, [arrays], core_ids=[0]).results[0]["out_0_dram"]
    return np.ascontiguousarray(result.transpose(1, 0, 2)).reshape(B, S, C)
```
